# Optimizing a Trainium2 kernel written in Bass

```python
import numpy as np
import jax
import jax.numpy as jnp

def _softmax(x, axis=-1):
    return jax.nn.softmax(x, axis=axis)
def _gelu(x):
    return jax.nn.gelu(x, approximate=True)
def _silu(x):
    return jax.nn.silu(x)
def _sigmoid(x):
    return jax.nn.sigmoid(x)
def _layernorm(x, axis=-1, eps=1e-5):
    m = jnp.mean(x, axis=axis, keepdims=True)
    v = jnp.var(x, axis=axis, keepdims=True)
    return (x - m) / jnp.sqrt(v + eps)
def _scatter_add(tgt, idx, src, axis=0):
    return tgt.at[idx].add(src)
def _segment_sum(src, seg, n):
    return jax.ops.segment_sum(src, seg, n)

kernel_name = 'mk_conv_seq_d1_conv_nchw256_07e6e9'

def setup_inputs(seed: int = 0):
    np.random.seed(seed)
    _w = jnp.asarray
    def _rec_inputs():
        import jax
        import jax.numpy as jnp
        _gk = jax.random.key(seed)
        x = -0.0002422 + 1 * jax.random.normal(jax.random.fold_in(_gk, 1), (64, 256, 64, 25), jnp.float32)
        return x
    x = _rec_inputs()
    def _L0_conv_setup():
        import jax, jax.numpy as jnp
        import numpy as np
        PSP_SIZES = (1, 4, 8, 16)

        def conv1x1(x, w, b):
            return jnp.einsum('bctv,oc->botv', x, w) + b[None, :, None, None]

        def psp(feats):
            n, c, t, v = feats.shape
            f = feats.reshape(n * v, c, t)
            outs = []
            for s in PSP_SIZES:
                p = f.reshape(n * v, c, s, t // s).mean(axis=-1)
                outs.append(p.reshape(n, c, s * v))
            return jnp.concatenate(outs, axis=-1)
        key = jax.random.key(seed)
        ks = jax.random.split(key, 8)
        B, C, T, V = (64, 256, 64, 25)
        C2 = C // 2
        std = 0.02
        return {'x': jax.random.normal(ks[0], (B, C, T, V), dtype=jnp.float32), 'g_w': jax.random.normal(ks[1], (C2, C), dtype=jnp.float32) * std, 'g_b': jnp.zeros((C2,), dtype=jnp.float32), 'theta_w': jax.random.normal(ks[2], (C2, C), dtype=jnp.float32) * std, 'theta_b': jnp.zeros((C2,), dtype=jnp.float32), 'W_w': jax.random.normal(ks[3], (C, C2), dtype=jnp.float32) * std, 'W_b': jnp.zeros((C,), dtype=jnp.float32), 'bn_gamma': jnp.ones((C,), dtype=jnp.float32), 'bn_beta': jnp.zeros((C,), dtype=jnp.float32), 'bn_mean': jnp.zeros((C,), dtype=jnp.float32), 'bn_var': jnp.ones((C,), dtype=jnp.float32)}
    _L0_conv_all = _L0_conv_setup()
    _L0_conv_in = {k: v for k, v in _L0_conv_all.items() if k in ('g_w', 'g_b', 'theta_w', 'theta_b', 'W_w', 'W_b', 'bn_gamma', 'bn_beta', 'bn_mean', 'bn_var', )}
    del _L0_conv_all

    return {
        "x": x,
        "L0_conv_g_w": _L0_conv_in["g_w"],
        "L0_conv_g_b": _L0_conv_in["g_b"],
        "L0_conv_theta_w": _L0_conv_in["theta_w"],
        "L0_conv_theta_b": _L0_conv_in["theta_b"],
        "L0_conv_W_w": _L0_conv_in["W_w"],
        "L0_conv_W_b": _L0_conv_in["W_b"],
        "L0_conv_bn_gamma": _L0_conv_in["bn_gamma"],
        "L0_conv_bn_beta": _L0_conv_in["bn_beta"],
        "L0_conv_bn_mean": _L0_conv_in["bn_mean"],
        "L0_conv_bn_var": _L0_conv_in["bn_var"],
    }

def reference(x, L0_conv_g_w, L0_conv_g_b, L0_conv_theta_w, L0_conv_theta_b, L0_conv_W_w, L0_conv_W_b, L0_conv_bn_gamma, L0_conv_bn_beta, L0_conv_bn_mean, L0_conv_bn_var):
    import jax
    import jax.numpy as jnp
    def _L0_conv_ref(x, g_w, g_b, theta_w, theta_b, W_w, W_b, bn_gamma, bn_beta, bn_mean, bn_var):
        import jax, jax.numpy as jnp
        import numpy as np
        PSP_SIZES = (1, 4, 8, 16)

        def conv1x1(x, w, b):
            return jnp.einsum('bctv,oc->botv', x, w) + b[None, :, None, None]

        def psp(feats):
            n, c, t, v = feats.shape
            f = feats.reshape(n * v, c, t)
            outs = []
            for s in PSP_SIZES:
                p = f.reshape(n * v, c, s, t // s).mean(axis=-1)
                outs.append(p.reshape(n, c, s * v))
            return jnp.concatenate(outs, axis=-1)
        B, C, T, V = x.shape
        C2 = C // 2
        eps = 1e-05
        g_x = psp(conv1x1(x, g_w, g_b))
        phi = g_x
        g_perm = jnp.swapaxes(g_x, 1, 2)
        theta = conv1x1(x, theta_w, theta_b).reshape(B, C2, T * V)
        theta = jnp.swapaxes(theta, 1, 2)
        f = jnp.einsum('bnc,bcs->bns', theta, phi)
        f = jax.nn.softmax(f, axis=-2)
        y = jnp.einsum('bns,bsc->bnc', f, g_perm)
        y = jax.nn.softmax(y, axis=-2)
        y = jnp.swapaxes(y, 1, 2).reshape(B, C2, T, V)
        y = conv1x1(y, W_w, W_b)
        z = y + x
        inv = jax.lax.rsqrt(bn_var + eps)
        z = (z - bn_mean[None, :, None, None]) * (inv * bn_gamma)[None, :, None, None] + bn_beta[None, :, None, None]
        return jax.nn.relu(z)

    def _gn(v, G=32, eps=1e-5):
        B_, C_, H_, W_ = v.shape
        g = v.reshape(B_, G, C_ // G, H_, W_)
        m = jnp.mean(g, axis=(2, 3, 4), keepdims=True)
        s = jnp.var(g, axis=(2, 3, 4), keepdims=True)
        return ((g - m) / jnp.sqrt(s + eps)).reshape(v.shape)

    def _ln_c(v, eps=1e-6):
        m = jnp.mean(v, axis=1, keepdims=True)
        s = jnp.var(v, axis=1, keepdims=True)
        return (v - m) / jnp.sqrt(s + eps)

    def _ln_t(v, eps=1e-5):
        m = jnp.mean(v, axis=-1, keepdims=True)
        s = jnp.var(v, axis=-1, keepdims=True)
        return (v - m) / jnp.sqrt(s + eps)

    def _to_tokens(v):
        B_, C_, H_, W_ = v.shape
        return v.reshape(B_, C_, H_ * W_).transpose(0, 2, 1)
    def _from_tokens(t, like):
        B_, C_, H_, W_ = like.shape
        return t.transpose(0, 2, 1).reshape(B_, C_, H_, W_)

    x = _L0_conv_ref(x, L0_conv_g_w, L0_conv_g_b, L0_conv_theta_w, L0_conv_theta_b, L0_conv_W_w, L0_conv_W_b, L0_conv_bn_gamma, L0_conv_bn_beta, L0_conv_bn_mean, L0_conv_bn_var)
    return x


_drawn_inputs = setup_inputs


def setup_inputs(seed=0):
    import zlib

    import numpy as np

    out = dict(_drawn_inputs(seed))
    spreads = {'L0_conv_g_b': (0.0, 0.8),
     'L0_conv_theta_b': (0.0, 0.1),
     'L0_conv_W_b': (0.0, 0.1),
     'L0_conv_bn_gamma': (1.0, 0.2),
     'L0_conv_bn_beta': (0.0, 0.1),
     'L0_conv_bn_mean': (0.0, 0.1),
     'L0_conv_bn_var': (1.0, 0.2)}
    factors = {'L0_conv_g_w': 8.0, 'L0_conv_theta_w': 8.0, 'L0_conv_W_w': 8.0}
    for name, (base, spread) in spreads.items():
        noise = np.random.default_rng([zlib.crc32(name.encode()), seed]).standard_normal(out[name].shape)
        drawn = base * np.exp(spread * noise) if base else spread * noise
        out[name] = jnp.asarray(drawn.astype(out[name].dtype))
    for name, factor in factors.items():
        out[name] = (out[name] * factor).astype(out[name].dtype)
    return out
```

```python
from contextlib import ExitStack

import concourse.bass as bass
from concourse import mybir

F32 = mybir.dt.float32
F32R = mybir.dt.float32r
ALU = mybir.AluOpType
ACT = mybir.ActivationFunctionType
AX = mybir.AxisListType

P = 128
POOLS = (1, 4, 8, 16)
BN_EPS = 1e-5
XBUFS = 3


def psp_nonlocal_kernel(nc, x, g_wT, g_b, theta_wT, theta_b, W_wT, bn_params, out):
    B, C, T, V = x.shape
    C2 = g_wT.shape[1]
    N = T * V
    CH = C // P
    assert C == CH * P and C2 == P and CH == 2
    NC = 4
    CW = N // NC
    S = V * sum(POOLS)
    ST = -(-S // P)
    SR = -(-S // ST)
    SP = ST * SR
    BANK = 512
    assert CW <= BANK and N == NC * CW

    level_at, at = {}, 0
    for s in POOLS:
        level_at[s] = (at, at + V * s)
        at += V * s
    COARSE = level_at[POOLS[-1]][0]
    FINE = V * POOLS[-1]

    ctx = ExitStack()
    with ctx:
        def sb(name, shape, dt=F32):
            return ctx.enter_context(nc.sbuf_tensor(name, shape, dt))

        def sem(name):
            return ctx.enter_context(nc.semaphore(name))

        x_ring = sb("x_ring", [P, XBUFS * CH, N])
        pair_sums = sb("pair_sums", [P, CH, N // 2])
        sums32 = sb("sums32", [P, CH, N // 32])
        pooled = sb("pooled", [P, CH, S])
        phi_hi = sb("phi_hi", [P, 2, SP], F32R)
        phi_lo = sb("phi_lo", [P, 2, SP], F32R)
        theta_hi = sb("theta_hi", [P, N], F32R)
        theta_lo = sb("theta_lo", [P, N], F32R)
        gT = sb("gT", [P, 2, ST * P])
        gT_scaled = sb("gT_scaled", [P, ST * P])
        probs = sb("probs", [P, 2, ST, N])
        neg_max = sb("neg_max", [P, ST])
        half_max = sb("half_max", [P, 2])
        zsum = sb("zsum", [P, ST])
        zinv = sb("zinv", [P, ST])
        y_sb = sb("y_sb", [P, N])
        ychunk_max = sb("ychunk_max", [P, NC])
        yneg_max = sb("yneg_max", [P, 1])
        yzsum = sb("yzsum", [P, 1])
        yzinv = sb("yzinv", [P, 1])
        o_sb = sb("o_sb", [P, CH, N])
        gw_sb = sb("gw_sb", [P, CH, C2])
        gw_level = sb("gw_level", [P, len(POOLS), CH, C2])
        tw_sb = sb("tw_sb", [P, CH, C2])
        Ww_sb = sb("Ww_sb", [P, C])
        Ww_scaled = sb("Ww_scaled", [P, C])
        gb_sb = sb("gb_sb", [P, 1])
        tb_sb = sb("tb_sb", [P, 1])
        bn = sb("bn", [P, 5, CH])
        bn_exp = sb("bn_exp", [P, CH])
        bn_inv = sb("bn_inv", [P, CH])
        bn_a = sb("bn_a", [P, CH])
        bn_c = sb("bn_c", [P, CH])
        ident = sb("ident", [P, P])
        ident_r = sb("ident_r", [P, P], F32R)

        f_ps = ctx.enter_context(nc.psum_tensor("f_ps", [P, NC, BANK], F32))
        pair_a = ctx.enter_context(nc.psum_tensor("pair_a", [P, 2, BANK], F32))
        pair_b = ctx.enter_context(nc.psum_tensor("pair_b", [P, 2, BANK], F32))
        pairs = (pair_a, pair_b)
        TPB = ST // 2
        assert ST % 2 == 0 and TPB * P <= BANK and FINE <= BANK and COARSE <= BANK

        x_landed = [sem("x_landed_even"), sem("x_landed_odd")]
        weights_landed = sem("weights_landed")
        ident_made = sem("ident_made")
        bn_step = sem("bn_step")
        consts_ready = sem("consts_ready")
        pads_cleared = sem("pads_cleared")
        pool_step = sem("pool_step")
        pooled_ready = sem("pooled_ready")
        g_ready = sem("g_ready")
        phi_hi_ready = sem("phi_hi_ready")
        phi_lo_ready = sem("phi_lo_ready")
        gT_ready = sem("gT_ready")
        gT_saved = sem("gT_saved")
        theta_ready = sem("theta_ready")
        theta_hi_ready = sem("theta_hi_ready")
        theta_lo_ready = sem("theta_lo_ready")
        f_ready = sem("f_ready")
        halves_ready = sem("halves_ready")
        max_ready = sem("max_ready")
        probs_ready = sem("probs_ready")
        zinv_ready = sem("zinv_ready")
        gT_scaled_ready = sem("gT_scaled_ready")
        y_ready = sem("y_ready")
        y_saved = sem("y_saved")
        ymax_ready = sem("ymax_ready")
        yexp_ready = sem("yexp_ready")
        yzinv_ready = sem("yzinv_ready")
        W_scaled_ready = sem("W_scaled_ready")
        o_ready = sem("o_ready")
        res_added = sem("res_added")
        relu_done = sem("relu_done")
        stored = [sem("stored_lower"), sem("stored_upper")]

        x_dram = x.rearrange("b (h p) t v -> b p h (t v)", p=P)
        out_dram = out.rearrange("b (h p) t v -> b h p (t v)", p=P)

        def x_of(b):
            return x_ring[:, bass.ds((b % XBUFS) * CH, CH), :]

        def x_half(b, h):
            return x_ring[:, bass.ds((b % XBUFS) * CH + h, 1), :].rearrange("p o n -> p (o n)")

        def chunk(c, n=1):
            return slice(c * CW, (c + n) * CW)

        def tile(t):
            return slice(t * SR, (t + 1) * SR)

        WEIGHT_DMAS = 6
        LAST = B - 1
        block = ctx.enter_context(nc.Block())

        @block.sync
        def _(sp):
            def load_x(b, parity):
                sp.dma_start(x_of(b), x_dram[b]).then_inc(x_landed[parity], 16)

            def store(b, h):
                sp.wait_ge(relu_done, 4 * b + 2 * h + 2)
                sp.dma_start(out_dram[b, h], o_sb[:, h, :]).then_inc(stored[h], 16)

            load_x(0, 0)
            load_x(1, 1)

            def store_and_load(p, parity):
                store(p - 1, 0)
                sp.wait_ge(res_added, 4 * p)
                load_x(p + 2, parity)
                store(p - 1, 1)

            sp.wait_ge(x_landed[0], 16)
            load_x(2, 0)
            with sp.Fori(1, LAST - 3, 2) as p:
                store_and_load(p, 1)
                store_and_load(p + 1, 0)
            store_and_load(LAST - 2, 1)
            for b in (LAST - 2, LAST - 1, LAST):
                for h in range(CH):
                    store(b, h)
            for h in range(CH):
                sp.wait_ge(stored[h], 16 * B)

        @block.gpsimd
        def _(pool):
            nc.gpsimd.memset(ident[:], 0.0).then_inc(pool_step, 1)
            nc.gpsimd.memset(bn_exp[:], -0.5).then_inc(pool_step, 1)
            pool.wait_ge(pool_step, 2)
            nc.gpsimd.affine_select(out=ident[:], in_=ident[:], compare_op=ALU.not_equal, fill=1.0, base=0,
                                    pattern=[[-1, P]], channel_multiplier=1).then_inc(ident_made, 1)
            pool.wait_ge(bn_step, 1)
            nc.gpsimd.tensor_tensor(bn_inv[:], bn_inv[:], bn_exp[:], ALU.pow).then_inc(bn_step, 1)
            SETUP_STEPS = 2
            STEPS = 5

            def add_pairs(dst, src):
                return nc.gpsimd.tensor_tensor(dst, src[:, :, 0::2], src[:, :, 1::2], ALU.add)

            def level(s):
                return pooled[:, :, level_at[s][0]:level_at[s][1]]

            def pool_batch(b, parity, loads):
                done = SETUP_STEPS + STEPS * b
                pool.wait_ge(x_landed[parity], 16 * loads)
                add_pairs(pair_sums[:], x_of(b)).then_inc(pool_step, 1)
                if type(b) is not int or b > 0:
                    pool.wait_ge(g_ready, b)
                pool.wait_ge(pool_step, done + 1)
                add_pairs(level(16), pair_sums).then_inc(pool_step, 1)
                pool.wait_ge(pool_step, done + 2)
                add_pairs(level(8), level(16)).then_inc(pool_step, 1)
                pool.wait_ge(pool_step, done + 3)
                add_pairs(level(4), level(8)).then_inc(pool_step, 1)
                pool.wait_ge(pool_step, done + 4)
                add_pairs(sums32[:], level(4)).then_inc(pool_step, 1)
                pool.wait_ge(pool_step, done + 5)
                add_pairs(level(1), sums32).then_inc(pooled_ready, 1)

            pool_batch(0, 0, 1)
            pool_batch(1, 1, 1)
            with pool.Fori(2, B, 2) as b:
                pool_batch(b, 0, b // 2 + 1)
                pool_batch(b + 1, 1, b // 2 + 1)

        @block.tensor
        def _(pe):
            def make_g(b):
                pe.wait_ge(pooled_ready, b + 1)
                for s in reversed(POOLS):
                    lo, hi = level_at[s]
                    li = POOLS.index(s)
                    dst = pair_b[:, 0, 0:FINE] if s == POOLS[-1] else pair_b[:, 1, lo:hi]
                    for h in range(CH):
                        mm = nc.tensor.matmul(dst, gw_level[:, li, h, :], pooled[:, h, lo:hi],
                                              start=(h == 0), stop=(h == CH - 1))
                mm.then_inc(g_ready, 1)

            def transpose_phi(b, parity):
                pe.wait_ge(phi_hi_ready, b + 1)
                pe.wait_ge(phi_lo_ready, b + 1)
                for t in range(ST):
                    dst = pair_b[0:SR, t // TPB, (t % TPB) * P:(t % TPB + 1) * P]
                    nc.tensor.matmul(dst, phi_hi[:, parity, tile(t)], ident_r[:], start=True, stop=False)
                    mm = nc.tensor.matmul(dst, phi_lo[:, parity, tile(t)], ident_r[:], start=False, stop=True)
                mm.then_inc(gT_ready, 1)

            def make_theta(b, pair):
                for c in range(2):
                    for h in range(CH):
                        cols = x_half(b, h)[:, chunk(2 * pair + c)]
                        mm = nc.tensor.matmul(pairs[pair][:, c, 0:CW], tw_sb[:, h, :], cols,
                                              start=(h == 0), stop=(h == CH - 1))
                mm.then_inc(theta_ready, 1)

            def scores(b, t, parity):
                if type(b) is not int or b + t > 0:
                    pe.wait_ge(probs_ready, ST * b + t)
                for c in range(NC):
                    if t == 0 and c % 2 == 0:
                        pe.wait_ge(theta_hi_ready, 2 * b + c // 2 + 1)
                        pe.wait_ge(theta_lo_ready, 2 * b + c // 2 + 1)
                    dst = f_ps[0:SR, c, 0:CW]
                    hi, lo = phi_hi[:, parity, tile(t)], phi_lo[:, parity, tile(t)]
                    nc.tensor.matmul(dst, hi, theta_hi[:, chunk(c)], start=True, stop=False)
                    nc.tensor.matmul(dst, hi, theta_lo[:, chunk(c)], start=False, stop=False)
                    mm = nc.tensor.matmul(dst, lo, theta_hi[:, chunk(c)], start=False, stop=True)
                    if c % 2 == 1:
                        mm.then_inc(f_ready, 1)

            def make_y(b, c, parity):
                if c == 0:
                    pe.wait_ge(gT_scaled_ready, b + 1)
                    if type(b) is not int or b > 0:
                        pe.wait_ge(res_added, 4 * b)
                if c >= 2:
                    pe.wait_ge(y_saved, 4 * b + c - 1)
                for t in range(ST):
                    mm = nc.tensor.matmul(pair_a[:, c % 2, 0:CW], gT_scaled[0:SR, t * P:(t + 1) * P],
                                          probs[0:SR, parity, t, chunk(c)], start=(t == 0), stop=(t == ST - 1))
                mm.then_inc(y_ready, 1)

            def make_out(b, k):
                h, pair = k // 2, k % 2
                if k >= 2:
                    pe.wait_ge(res_added, 4 * b + k - 1)
                for c in range(2):
                    mm = nc.tensor.matmul(pairs[pair][:, c, 0:CW], Ww_scaled[:, h * P:(h + 1) * P],
                                          y_sb[:, chunk(2 * pair + c)], start=True, stop=True)
                mm.then_inc(o_ready, 1)

            def phase(p, parity, with_last=True, with_next=True):
                for t in range(ST):
                    scores(p, t, parity)
                    if with_last and t < NC:
                        make_y(p - 1, t, 1 - parity)
                    if with_next and t == ST - 2:
                        make_g(p + 1)
                convolve_and_out(p, parity, with_last, with_next)

            def convolve_and_out(p, parity, with_last, with_next):
                if with_next:
                    transpose_phi(p + 1, 1 - parity)
                    if with_last:
                        pe.wait_ge(y_saved, 4 * p)
                    make_theta(p + 1, 0)
                    pe.wait_ge(gT_saved, p + 2)
                    make_theta(p + 1, 1)
                if with_last:
                    pe.wait_ge(yexp_ready, p)
                    pe.wait_ge(W_scaled_ready, p)
                    for k in range(4):
                        if k < 2 and with_next:
                            pe.wait_ge(theta_hi_ready, 2 * (p + 1) + k + 1)
                            pe.wait_ge(theta_lo_ready, 2 * (p + 1) + k + 1)
                        make_out(p - 1, k)

            pe.wait_ge(consts_ready, 3)
            pe.wait_ge(x_landed[0], 16)
            make_g(0)
            convolve_and_out(-1, 1, False, True)
            phase(0, 0, with_last=False)
            phase(1, 1)
            phase(2, 0)
            with pe.Fori(3, LAST, 2) as p:
                phase(p, 1)
                phase(p + 1, 0)
            phase(LAST, LAST % 2, with_next=False)
            for c in range(NC):
                make_y(LAST, c, LAST % 2)
            convolve_and_out(B, 0, True, False)

        @block.scalar
        def _(act):
            act.dma_start(gw_sb[:], g_wT.rearrange("(h p) o -> p h o", p=P)).then_inc(weights_landed, 16)
            act.dma_start(tw_sb[:], theta_wT.rearrange("(h p) o -> p h o", p=P)).then_inc(weights_landed, 16)
            act.dma_start(Ww_sb[:], W_wT).then_inc(weights_landed, 16)
            act.dma_start(gb_sb[:], g_b.rearrange("(p o) -> p o", o=1)).then_inc(weights_landed, 16)
            act.dma_start(tb_sb[:], theta_b.rearrange("(p o) -> p o", o=1)).then_inc(weights_landed, 16)
            act.dma_start(bn[:], bn_params).then_inc(weights_landed, 16)
            act.wait_ge(weights_landed, 16 * WEIGHT_DMAS)
            for li, s in enumerate(POOLS):
                last = nc.scalar.mul(gw_level[:, li, :, :], gw_sb[:], float(s) / T)
            last.then_inc(consts_ready, 1)
            act.wait_ge(ident_made, 1)
            nc.scalar.copy(ident_r[:], ident[:]).then_inc(consts_ready, 1)

            def save_phi_hi(b, parity):
                act.wait_ge(g_ready, b + 1)
                nc.scalar.activation(phi_hi[:, parity, COARSE:S], pair_b[:, 0, 0:FINE], ACT.Identity,
                                     bias=gb_sb[:, 0:1])
                nc.scalar.activation(phi_hi[:, parity, 0:COARSE], pair_b[:, 1, 0:COARSE], ACT.Identity,
                                     bias=gb_sb[:, 0:1]).then_inc(phi_hi_ready, 1)

            def save_gT(b, parity):
                act.wait_ge(gT_ready, b + 1)
                nc.scalar.copy(gT[0:SR, parity, :].rearrange("p (a n) -> p a n", a=2),
                               pair_b[0:SR, :, 0:TPB * P]).then_inc(gT_saved, 1)

            def save_theta_hi(b, pair):
                act.wait_ge(theta_ready, 2 * b + pair + 1)
                nc.scalar.activation(theta_hi[:, chunk(2 * pair, 2)].rearrange("p (c n) -> p c n", c=2),
                                     pairs[pair][:, :, 0:CW], ACT.Identity,
                                     bias=tb_sb[:, 0:1]).then_inc(theta_hi_ready, 1)

            def exponentials(b, t, parity):
                act.wait_ge(max_ready, ST * b + t + 1)
                nc.scalar.activation(probs[0:SR, parity, t, :].rearrange("p (c n) -> p c n", c=NC),
                                     f_ps[0:SR, :, 0:CW], ACT.Exp, bias=neg_max[0:SR, t:t + 1],
                                     accum_out=zsum[0:SR, t:t + 1]).then_inc(probs_ready, 1)

            def y_exponentials(b):
                act.wait_ge(ymax_ready, b + 1)
                nc.scalar.activation(y_sb[:], y_sb[:], ACT.Exp, bias=yneg_max[:, 0:1],
                                     accum_out=yzsum[:, 0:1]).then_inc(yexp_ready, 1)

            def relu(b, k):
                h, pair = k // 2, k % 2
                act.wait_ge(res_added, 4 * b + k + 1)
                cols = o_sb[:, h, chunk(2 * pair, 2)]
                nc.scalar.activation(cols, cols, ACT.Relu, bias=bn_c[:, h:h + 1],
                                     scale=bn_a[:, h:h + 1]).then_inc(relu_done, 1)

            def phase(p, parity, with_last=True, with_next=True):
                for t in range(ST):
                    if t == ST - 1 and with_next:
                        save_gT(p + 1, 1 - parity)
                    exponentials(p, t, parity)
                    if with_last and t == NC - 1:
                        y_exponentials(p - 1)
                    if with_next and t == ST - 2:
                        save_phi_hi(p + 1, 1 - parity)
                if with_next:
                    for pair in range(2):
                        save_theta_hi(p + 1, pair)
                if with_last:
                    for k in range(4):
                        relu(p - 1, k)

            act.wait_ge(pads_cleared, 2)
            save_phi_hi(0, 0)
            save_gT(0, 0)
            for pair in range(2):
                save_theta_hi(0, pair)
            phase(0, 0, with_last=False)
            act.wait_ge(consts_ready, 3)
            with act.Fori(1, LAST, 2) as p:
                phase(p, 1)
                phase(p + 1, 0)
            phase(LAST, LAST % 2, with_next=False)
            y_exponentials(LAST)
            for k in range(4):
                relu(LAST, k)

        @block.vector
        def _(dve):
            if SP > S:
                nc.vector.memset(phi_hi[:, :, S:SP].bitcast(F32), 0.0).then_inc(pads_cleared, 1)
                nc.vector.memset(phi_lo[:, :, S:SP].bitcast(F32), 0.0).then_inc(pads_cleared, 1)
            dve.wait_ge(weights_landed, 16 * WEIGHT_DMAS)
            nc.vector.tensor_scalar(bn_inv[:], bn[:, 4, :], BN_EPS, None, ALU.add).then_inc(bn_step, 1)
            dve.wait_ge(bn_step, 2)
            nc.vector.tensor_tensor(bn_a[:], bn_inv[:], bn[:, 1, :], ALU.mult).then_inc(bn_step, 1)
            nc.vector.tensor_tensor(bn_c[:], bn[:, 0, :], bn[:, 3, :], ALU.subtract).then_inc(bn_step, 1)
            dve.wait_ge(bn_step, 4)
            nc.vector.tensor_tensor(bn_c[:], bn_c[:], bn_a[:], ALU.mult).then_inc(bn_step, 1)
            dve.wait_ge(bn_step, 5)
            nc.vector.tensor_tensor(bn_c[:], bn_c[:], bn[:, 2, :], ALU.add).then_inc(consts_ready, 1)

            def low_part(dst, psum, bias, hi):
                return nc.vector.scalar_tensor_tensor(out=dst, in0=psum, scalar=bias, in1=hi,
                                                      op0=ALU.add, op1=ALU.subtract)

            def save_phi_lo(b, parity):
                dve.wait_ge(phi_hi_ready, b + 1)
                low_part(phi_lo[:, parity, COARSE:S], pair_b[:, 0, 0:FINE], gb_sb[:, 0:1],
                         phi_hi[:, parity, COARSE:S].bitcast(F32))
                low_part(phi_lo[:, parity, 0:COARSE], pair_b[:, 1, 0:COARSE], gb_sb[:, 0:1],
                         phi_hi[:, parity, 0:COARSE].bitcast(F32)).then_inc(phi_lo_ready, 1)

            def save_theta_lo(b, pair):
                dve.wait_ge(theta_hi_ready, 2 * b + pair + 1)
                low_part(theta_lo[:, chunk(2 * pair, 2)].rearrange("p (c n) -> p c n", c=2),
                         pairs[pair][:, :, 0:CW], tb_sb[:, 0:1],
                         theta_hi[:, chunk(2 * pair, 2)].bitcast(F32).rearrange("p (c n) -> p c n", c=2)
                         ).then_inc(theta_lo_ready, 1)

            def maxima(b, t):
                for half in range(2):
                    dve.wait_ge(f_ready, 2 * (ST * b + t) + half + 1)
                    nc.vector.tensor_reduce(half_max[0:SR, half:half + 1],
                                            f_ps[0:SR, 2 * half:2 * half + 2, 0:CW], AX.XY, ALU.max,
                                            negate=True).then_inc(halves_ready, 1)
                dve.wait_ge(halves_ready, 2 * (ST * b + t + 1))
                nc.vector.tensor_tensor(neg_max[0:SR, t:t + 1], half_max[0:SR, 0:1], half_max[0:SR, 1:2],
                                        ALU.min).then_inc(max_ready, 1)

            def save_y(b, c):
                dve.wait_ge(y_ready, 4 * b + c + 1)
                if c == 0 and (type(b) is not int or b > 0):
                    dve.wait_ge(o_ready, 4 * b)
                nc.vector.tensor_scalar(y_sb[:, chunk(c)], pair_a[:, c % 2, 0:CW], 1.0, None, ALU.mult,
                                        ALU.max, accum_out=ychunk_max[:, c:c + 1]).then_inc(y_saved, 1)

            def y_maximum(b):
                dve.wait_ge(y_saved, 4 * b + 4)
                nc.vector.tensor_reduce(yneg_max[:, 0:1], ychunk_max[:], AX.X, ALU.max,
                                        negate=True).then_inc(ymax_ready, 1)

            def scale_W(b):
                dve.wait_ge(yexp_ready, b + 1)
                nc.vector.reciprocal(yzinv[:, 0:1], yzsum[:, 0:1]).then_inc(yzinv_ready, 1)
                dve.wait_ge(yzinv_ready, b + 1)
                nc.vector.tensor_scalar(Ww_scaled[:], Ww_sb[:], yzinv[:, 0:1], None,
                                        ALU.mult).then_inc(W_scaled_ready, 1)

            def scale_gT(b, parity):
                dve.wait_ge(probs_ready, ST * (b + 1))
                nc.vector.reciprocal(zinv[0:SR, :], zsum[0:SR, :]).then_inc(zinv_ready, 1)
                dve.wait_ge(gT_saved, b + 1)
                dve.wait_ge(zinv_ready, b + 1)
                for t in range(ST):
                    cols = slice(t * P, (t + 1) * P)
                    last = nc.vector.tensor_scalar(gT_scaled[0:SR, cols], gT[0:SR, parity, cols],
                                                   zinv[0:SR, t:t + 1], None, ALU.mult)
                last.then_inc(gT_scaled_ready, 1)

            def residual(b, k):
                h, pair = k // 2, k % 2
                dve.wait_ge(o_ready, 4 * b + k + 1)
                if k % 2 == 0 and (type(b) is not int or b > 0):
                    dve.wait_ge(stored[h], 16 * b)
                nc.vector.tensor_tensor(
                    o_sb[:, h, chunk(2 * pair, 2)].rearrange("p (c n) -> p c n", c=2),
                    pairs[pair][:, :, 0:CW],
                    x_half(b, h)[:, chunk(2 * pair, 2)].rearrange("p (c n) -> p c n", c=2),
                    ALU.add).then_inc(res_added, 1)

            def phase(p, parity, with_last=True, with_next=True):
                for t in range(ST):
                    maxima(p, t)
                    if with_last and t < NC:
                        save_y(p - 1, t)
                    if with_last and t == NC - 1:
                        y_maximum(p - 1)
                    if t == ST - 2:
                        if with_last:
                            scale_W(p - 1)
                        if with_next:
                            save_phi_lo(p + 1, 1 - parity)
                if with_next:
                    for pair in range(2):
                        save_theta_lo(p + 1, pair)
                scale_gT(p, parity)
                if with_last:
                    for k in range(4):
                        residual(p - 1, k)

            save_phi_lo(0, 0)
            for pair in range(2):
                save_theta_lo(0, pair)
            phase(0, 0, with_last=False)
            phase(1, 1)
            phase(2, 0)
            with dve.Fori(3, LAST, 2) as p:
                phase(p, 1)
                phase(p + 1, 0)
            phase(LAST, LAST % 2, with_next=False)
            for c in range(NC):
                save_y(LAST, c)
            y_maximum(LAST)
            scale_W(LAST)
            for k in range(4):
                residual(LAST, k)


_BN_PARAMS = ("W_b", "bn_gamma", "bn_beta", "bn_mean", "bn_var")


def kernel(**inputs):
    import numpy as _np
    import concourse.bacc as _bacc
    from concourse import mybir as _mybir
    from concourse.bass_utils import run_bass_kernel_spmd as _run

    nc = _bacc.Bacc("TRN2", target_bir_lowering=False, num_devices=1)
    arrays = {"x": _np.ascontiguousarray(inputs["x"])}
    for name in ("g_w", "theta_w", "W_w"):
        arrays[name + "T"] = _np.ascontiguousarray(_np.asarray(inputs["L0_conv_" + name]).T)
    for name in ("g_b", "theta_b"):
        arrays[name] = _np.ascontiguousarray(inputs["L0_conv_" + name])
    stacked = _np.stack([_np.asarray(inputs["L0_conv_" + name]) for name in _BN_PARAMS])
    arrays["bn_params"] = _np.ascontiguousarray(stacked.reshape(len(_BN_PARAMS), -1, P).transpose(2, 0, 1))
    aps = {n: nc.dram_tensor("in_" + n, a.shape, _mybir.dt.from_np(a.dtype), kind="ExternalInput").ap()
           for n, a in arrays.items()}
    out = nc.dram_tensor("out", arrays["x"].shape, _mybir.dt.float32, kind="ExternalOutput").ap()
    psp_nonlocal_kernel(nc, aps["x"], aps["g_wT"], aps["g_b"], aps["theta_wT"], aps["theta_b"], aps["W_wT"],
                        aps["bn_params"], out)
    r = _run(nc, [{"in_" + n: a for n, a in arrays.items()}], core_ids=[0])
    return r.results[0]["out"]
```

```python
from contextlib import ExitStack

import concourse.bass as bass
from concourse import mybir

F32 = mybir.dt.float32
F32R = mybir.dt.float32r
ALU = mybir.AluOpType
ACT = mybir.ActivationFunctionType
AX = mybir.AxisListType

P = 128
POOLS = (1, 4, 8, 16)
BN_EPS = 1e-5
XHALVES = 7


def psp_nonlocal_kernel(nc, x, g_wT, g_b, theta_wT, theta_b, W_wT, bn_params, out):
    B, C, T, V = x.shape
    C2 = g_wT.shape[1]
    N = T * V
    CH = C // P
    assert C == CH * P and C2 == P and CH == 2
    NC = 4
    CW = N // NC
    S = V * sum(POOLS)
    ST = -(-S // P)
    SR = -(-S // ST)
    SP = ST * SR
    GT = 2
    GC = ST // GT
    GROUPS = NC * GC
    SLOTS = 4
    DVE_GROUPS = (4, 7, 10)
    EARLY = 4
    BANK = 512
    assert CW <= BANK and N == NC * CW and ST == GC * GT and GROUPS % SLOTS == 0

    level_at, at = {}, 0
    for s in POOLS:
        level_at[s] = (at, at + V * s)
        at += V * s
    COARSE = level_at[POOLS[-1]][0]
    FINE = V * POOLS[-1]

    ctx = ExitStack()
    with ctx:
        def sb(name, shape, dt=F32):
            return ctx.enter_context(nc.sbuf_tensor(name, shape, dt))

        def sem(name):
            return ctx.enter_context(nc.semaphore(name))

        x_ring = sb("x_ring", [P, XHALVES, N])
        pair_sums = sb("pair_sums", [P, CH, N // 2])
        sums32 = sb("sums32", [P, CH, N // 32])
        pooled = sb("pooled", [P, CH, S])
        phi_hi = sb("phi_hi", [P, 2, SP], F32R)
        phi_lo = sb("phi_lo", [P, 2, SP], F32R)
        theta_hi = sb("theta_hi", [P, N], F32R)
        theta_lo = sb("theta_lo", [P, N], F32R)
        gT = sb("gT", [P, 2, ST * P])
        gT_hi = sb("gT_hi", [P, ST * P], F32R)
        gT_lo = sb("gT_lo", [P, ST * P], F32R)
        probs = sb("probs", [P, 2, ST, N])
        probs_hi = sb("probs_hi", [P, SLOTS, GT, CW], F32R)
        probs_lo = sb("probs_lo", [P, SLOTS, GT, CW], F32R)
        neg_max = sb("neg_max", [P, ST])
        half_max = sb("half_max", [P, 2])
        zhalf = sb("zhalf", [P, 2, ST])
        zsum = sb("zsum", [P, ST])
        zinv = sb("zinv", [P, ST])
        y_sb = sb("y_sb", [P, N])
        ychunk_max = sb("ychunk_max", [P, NC])
        yneg_max = sb("yneg_max", [P, 1])
        yzsum = sb("yzsum", [P, 1])
        yzinv = sb("yzinv", [P, 1])
        gw_sb = sb("gw_sb", [P, CH, C2])
        gw_level = sb("gw_level", [P, len(POOLS), CH, C2])
        tw_sb = sb("tw_sb", [P, CH, C2])
        Ww_sb = sb("Ww_sb", [P, C])
        Ww_scaled = sb("Ww_scaled", [P, C])
        gb_sb = sb("gb_sb", [P, 1])
        tb_sb = sb("tb_sb", [P, 1])
        bn = sb("bn", [P, 5, CH])
        bn_exp = sb("bn_exp", [P, CH])
        bn_inv = sb("bn_inv", [P, CH])
        bn_a = sb("bn_a", [P, CH])
        bn_c = sb("bn_c", [P, CH])
        ident = sb("ident", [P, P])
        ident_r = sb("ident_r", [P, P], F32R)

        f_ps = ctx.enter_context(nc.psum_tensor("f_ps", [P, NC, BANK], F32))
        pair_a = ctx.enter_context(nc.psum_tensor("pair_a", [P, 2, BANK], F32))
        pair_b = ctx.enter_context(nc.psum_tensor("pair_b", [P, 2, BANK], F32))
        f_back = f_ps[:, 2:4, :]
        theta_ps = (pair_b, pair_a)
        g_ps = pair_a
        out_ps = (pair_b, f_back, pair_b, pair_a)
        TPB = ST // 2
        assert ST % 2 == 0 and TPB * P <= BANK and FINE <= BANK and COARSE <= BANK

        x_landed = [[sem(f"x_landed_{parity}_{h}") for h in range(CH)] for parity in ("even", "odd")]
        weights_landed = sem("weights_landed")
        ident_made = sem("ident_made")
        bn_step = sem("bn_step")
        consts_ready = sem("consts_ready")
        pads_cleared = sem("pads_cleared")
        pool_step = sem("pool_step")
        pair_upper_ready = sem("pair_upper_ready")
        pooled_ready = sem("pooled_ready")
        g_ready = sem("g_ready")
        phi_hi_ready = sem("phi_hi_ready")
        phi_lo_ready = sem("phi_lo_ready")
        gT_ready = sem("gT_ready")
        gT_saved = sem("gT_saved")
        theta_ready = sem("theta_ready")
        theta_hi_ready = sem("theta_hi_ready")
        theta_lo_ready = sem("theta_lo_ready")
        f_ready = sem("f_ready")
        halves_ready = sem("halves_ready")
        max_ready = sem("max_ready")
        probs_ready = sem("probs_ready")
        zsum_ready = sem("zsum_ready")
        zinv_ready = sem("zinv_ready")
        gT_hi_step = sem("gT_hi_step")
        gT_parts_ready = sem("gT_parts_ready")
        group_hi_ready = sem("group_hi_ready")
        group_lo_ready = sem("group_lo_ready")
        group_lo_ready_dve = sem("group_lo_ready_dve")
        group_used = sem("group_used")
        y_saved = sem("y_saved")
        ymax_ready = sem("ymax_ready")
        yexp_ready = sem("yexp_ready")
        yzinv_ready = sem("yzinv_ready")
        W_scaled_ready = sem("W_scaled_ready")
        o_ready = sem("o_ready")
        res_added = sem("res_added")
        relu_done = sem("relu_done")
        stored = [sem("stored_lower"), sem("stored_upper")]

        x_dram = x.rearrange("b (h p) t v -> b p h (t v)", p=P)
        out_dram = out.rearrange("b (h p) t v -> b h p (t v)", p=P)

        def x_half(b, h):
            return x_ring[:, bass.ds((CH * b + h) % XHALVES, 1), :].rearrange("p o n -> p (o n)")

        def chunk(c, n=1):
            return slice(c * CW, (c + n) * CW)

        def tile(t):
            return slice(t * SR, (t + 1) * SR)

        def group_of(g, parity):
            t = GT * (g % GC)
            return probs[0:SR, parity, t:t + GT, chunk(g // GC)]

        WEIGHT_DMAS = 6
        LAST = B - 1
        block = ctx.enter_context(nc.Block())

        @block.sync
        def _(sp):
            BACK = [-(-(XHALVES - h) // CH) for h in range(CH)]
            FREES = [(h - XHALVES) % CH for h in range(CH)]

            def load_x(b, h, parity):
                if type(b) is not int or b >= BACK[h]:
                    sp.wait_ge(stored[FREES[h]], 16 * (b - BACK[h] + 1))
                sp.dma_start(x_half(b, h), x_dram[b, :, h]).then_inc(x_landed[parity][h], 16)

            def store(b, h):
                sp.wait_ge(relu_done, 4 * b + 2 * h + 2)
                sp.dma_start(out_dram[b, h], x_half(b, h)).then_inc(stored[h], 16)

            for b in range(2):
                for h in range(CH):
                    load_x(b, h, b)
            for h in range(CH):
                sp.wait_ge(x_landed[0][h], 16)
                load_x(2, h, 0)
            sp.wait_ge(x_landed[1][0], 16)
            load_x(3, 0, 1)

            def store_and_load(p, parity):
                store(p - 1, 0)
                load_x(p + 2, 1, parity)
                store(p - 1, 1)
                load_x(p + 3, 0, 1 - parity)

            with sp.Fori(1, LAST - 3, 2) as p:
                store_and_load(p, 1)
                store_and_load(p + 1, 0)
            store(LAST - 3, 0)
            load_x(LAST, 1, LAST % 2)
            store(LAST - 3, 1)
            for b in (LAST - 2, LAST - 1, LAST):
                for h in range(CH):
                    store(b, h)
            for h in range(CH):
                sp.wait_ge(stored[h], 16 * B)

        @block.gpsimd
        def _(pool):
            nc.gpsimd.memset(ident[:], 0.0).then_inc(pool_step, 1)
            nc.gpsimd.memset(bn_exp[:], -0.5).then_inc(pool_step, 1)
            pool.wait_ge(pool_step, 2)
            nc.gpsimd.affine_select(out=ident[:], in_=ident[:], compare_op=ALU.not_equal, fill=1.0, base=0,
                                    pattern=[[-1, P]], channel_multiplier=1).then_inc(ident_made, 1)
            pool.wait_ge(bn_step, 1)
            nc.gpsimd.tensor_tensor(bn_inv[:], bn_inv[:], bn_exp[:], ALU.pow).then_inc(bn_step, 1)
            SETUP_STEPS = 2
            STEPS = 5

            def add_pairs(dst, src):
                return nc.gpsimd.tensor_tensor(dst, src[:, :, 0::2], src[:, :, 1::2], ALU.add)

            def level(s):
                return pooled[:, :, level_at[s][0]:level_at[s][1]]

            def pair_lower(b, parity, turn):
                pool.wait_ge(x_landed[parity][0], 16 * turn)
                if type(b) is not int or b > 0:
                    pool.wait_ge(pool_step, SETUP_STEPS + STEPS * (b - 1) + 2)
                src = x_half(b, 0)
                nc.gpsimd.tensor_tensor(pair_sums[:, 0, :], src[:, 0::2], src[:, 1::2],
                                        ALU.add).then_inc(pool_step, 1)

            def pool_batch(b):
                done = SETUP_STEPS + STEPS * b
                if type(b) is not int or b > 0:
                    pool.wait_ge(g_ready, b)
                pool.wait_ge(pool_step, done + 1)
                pool.wait_ge(pair_upper_ready, b + 1)
                add_pairs(level(16), pair_sums).then_inc(pool_step, 1)
                pool.wait_ge(pool_step, done + 2)
                add_pairs(level(8), level(16)).then_inc(pool_step, 1)
                pool.wait_ge(pool_step, done + 3)
                add_pairs(level(4), level(8)).then_inc(pool_step, 1)
                pool.wait_ge(pool_step, done + 4)
                add_pairs(sums32[:], level(4)).then_inc(pool_step, 1)
                pool.wait_ge(pool_step, done + 5)
                add_pairs(level(1), sums32).then_inc(pooled_ready, 1)

            def group_lo(b, g, parity):
                if g in DVE_GROUPS:
                    return
                pool.wait_ge(group_hi_ready, GROUPS * b + g + 1)
                nc.gpsimd.tensor_tensor(probs_lo[0:SR, g % SLOTS], group_of(g, parity),
                                        probs_hi[0:SR, g % SLOTS].bitcast(F32),
                                        ALU.subtract).then_inc(group_lo_ready, 1)

            def phase(p, parity, turn, with_last=True, with_next=True):
                if with_next:
                    pair_lower(p + 1, 1 - parity, turn)
                if with_last:
                    for g in range(SLOTS, GROUPS):
                        group_lo(p - 1, g, 1 - parity)
                if with_next:
                    pool_batch(p + 1)
                for g in range(SLOTS):
                    group_lo(p, g, parity)

            pair_lower(0, 0, 1)
            pool_batch(0)
            phase(0, 0, 1, with_last=False)
            with pool.Fori(1, LAST, 2) as p:
                phase(p, 1, (p + 1) // 2 + 1)
                phase(p + 1, 0, (p + 1) // 2 + 1)
            phase(LAST, LAST % 2, 0, with_next=False)
            for g in range(SLOTS, GROUPS):
                group_lo(LAST, g, LAST % 2)

        @block.tensor
        def _(pe):
            def make_g(b):
                pe.wait_ge(pooled_ready, b + 1)
                for s in reversed(POOLS):
                    lo, hi = level_at[s]
                    li = POOLS.index(s)
                    dst = g_ps[:, 0, 0:FINE] if s == POOLS[-1] else g_ps[:, 1, lo:hi]
                    for h in range(CH):
                        mm = nc.tensor.matmul(dst, gw_level[:, li, h, :], pooled[:, h, lo:hi],
                                              start=(h == 0), stop=(h == CH - 1))
                mm.then_inc(g_ready, 1)

            def transpose_phi(b, parity):
                for t in range(ST):
                    dst = f_ps[0:SR, t // TPB, (t % TPB) * P:(t % TPB + 1) * P]
                    nc.tensor.matmul(dst, phi_hi[:, parity, tile(t)], ident_r[:], start=True, stop=False)
                    mm = nc.tensor.matmul(dst, phi_lo[:, parity, tile(t)], ident_r[:], start=False, stop=True)
                mm.then_inc(gT_ready, 1)

            def make_theta(b, pair):
                for c in range(2):
                    for h in range(CH):
                        cols = x_half(b, h)[:, chunk(2 * pair + c)]
                        mm = nc.tensor.matmul(theta_ps[pair][:, c, 0:CW], tw_sb[:, h, :], cols,
                                              start=(h == 0), stop=(h == CH - 1))
                mm.then_inc(theta_ready, 1)

            def scores(b, t, parity):
                for c in range(NC):
                    if t > 0 and c % 2 == 0:
                        pe.wait_ge(probs_ready, 2 * (ST * b + t - 1) + c // 2 + 1)
                    if t == 0 and c == 0:
                        pe.wait_ge(gT_saved, b + 1)
                    if t == 0 and c == 2 and (type(b) is not int or b > 1):
                        pe.wait_ge(res_added, 4 * (b - 2) + 2)
                    if t == 0 and c % 2 == 0:
                        pe.wait_ge(theta_hi_ready, 2 * b + c // 2 + 1)
                        pe.wait_ge(theta_lo_ready, 2 * b + c // 2 + 1)
                    dst = f_ps[0:SR, c, 0:CW]
                    hi, lo = phi_hi[:, parity, tile(t)], phi_lo[:, parity, tile(t)]
                    nc.tensor.matmul(dst, hi, theta_hi[:, chunk(c)], start=True, stop=False)
                    nc.tensor.matmul(dst, hi, theta_lo[:, chunk(c)], start=False, stop=False)
                    mm = nc.tensor.matmul(dst, lo, theta_hi[:, chunk(c)], start=False, stop=True)
                    if c % 2 == 1:
                        mm.then_inc(f_ready, 1)

            def make_y(b, c):
                if c == 0:
                    pe.wait_ge(gT_parts_ready, b + 1)
                    if type(b) is not int or b > 0:
                        pe.wait_ge(res_added, 4 * b)
                if c >= 2:
                    pe.wait_ge(y_saved, 4 * b + c - 1)
                for q in range(GC):
                    g = GC * c + q
                    pe.wait_ge(group_hi_ready, GROUPS * b + g + 1)
                    if g in DVE_GROUPS:
                        pe.wait_ge(group_lo_ready_dve, len(DVE_GROUPS) * b + DVE_GROUPS.index(g) + 1)
                    else:
                        before = sum(q < g for q in range(GROUPS) if q not in DVE_GROUPS)
                        pe.wait_ge(group_lo_ready, (GROUPS - len(DVE_GROUPS)) * b + before + 1)
                    for i in range(GT):
                        t = GT * q + i
                        dst = pair_a[:, c % 2, 0:CW]
                        hi, lo = gT_hi[0:SR, t * P:(t + 1) * P], gT_lo[0:SR, t * P:(t + 1) * P]
                        p_hi, p_lo = probs_hi[0:SR, g % SLOTS, i], probs_lo[0:SR, g % SLOTS, i]
                        nc.tensor.matmul(dst, hi, p_hi, start=(t == 0), stop=False)
                        nc.tensor.matmul(dst, lo, p_hi, start=False, stop=False)
                        mm = nc.tensor.matmul(dst, hi, p_lo, start=False, stop=(t == ST - 1))
                    mm.then_inc(group_used, 1)

            def make_out(b, k):
                h, pair = k // 2, k % 2
                for c in range(2):
                    mm = nc.tensor.matmul(out_ps[k][:, c, 0:CW], Ww_scaled[:, h * P:(h + 1) * P],
                                          y_sb[:, chunk(2 * pair + c)], start=True, stop=True)
                mm.then_inc(o_ready, 1)

            def end_of_phase(p, parity, with_last, with_next):
                if with_next:
                    pe.wait_ge(phi_hi_ready, 2 * (p + 2))
                    pe.wait_ge(phi_lo_ready, p + 2)
                    make_theta(p + 1, 1)
                if with_last:
                    pe.wait_ge(yexp_ready, p)
                    pe.wait_ge(W_scaled_ready, p)
                    if with_next:
                        pe.wait_ge(theta_hi_ready, 2 * (p + 1) + 1)
                        pe.wait_ge(theta_lo_ready, 2 * (p + 1) + 1)
                    make_out(p - 1, 0)
                if (type(p) is not int or 0 <= p < B):
                    pe.wait_ge(probs_ready, 2 * ST * (p + 1))
                if with_last:
                    make_out(p - 1, 1)
                if with_next:
                    transpose_phi(p + 1, 1 - parity)
                if with_last:
                    pe.wait_ge(res_added, 4 * (p - 1) + 1)
                    make_out(p - 1, 2)
                    if with_next:
                        pe.wait_ge(theta_hi_ready, 2 * (p + 1) + 2)
                        pe.wait_ge(theta_lo_ready, 2 * (p + 1) + 2)
                    make_out(p - 1, 3)

            def phase(p, parity, turn=0, with_last=True, with_next=True):
                for t in range(ST):
                    scores(p, t, parity)
                    if with_last and t < NC:
                        make_y(p - 1, t)
                    if with_next and t == NC:
                        for h in range(CH):
                            pe.wait_ge(x_landed[1 - parity][h], 16 * turn)
                        if type(p) is not int or p > 1:
                            pe.wait_ge(res_added, 4 * (p - 2) + 3)
                        make_theta(p + 1, 0)
                        if with_last:
                            pe.wait_ge(y_saved, 4 * p)
                        make_g(p + 1)
                end_of_phase(p, parity, with_last, with_next)

            pe.wait_ge(consts_ready, 3)
            for h in range(CH):
                pe.wait_ge(x_landed[0][h], 16)
            make_theta(0, 0)
            make_g(0)
            end_of_phase(-1, 1, False, True)
            phase(0, 0, 1, with_last=False)
            phase(1, 1, 2)
            phase(2, 0, 2)
            with pe.Fori(3, LAST, 2) as p:
                phase(p, 1, (p + 1) // 2 + 1)
                phase(p + 1, 0, (p + 1) // 2 + 1)
            phase(LAST, LAST % 2, with_next=False)
            for c in range(NC):
                make_y(LAST, c)
            pe.wait_ge(y_saved, 4 * B)
            end_of_phase(B, 0, True, False)

        @block.scalar
        def _(act):
            act.dma_start(gw_sb[:], g_wT.rearrange("(h p) o -> p h o", p=P)).then_inc(weights_landed, 16)
            act.dma_start(tw_sb[:], theta_wT.rearrange("(h p) o -> p h o", p=P)).then_inc(weights_landed, 16)
            act.dma_start(Ww_sb[:], W_wT).then_inc(weights_landed, 16)
            act.dma_start(gb_sb[:], g_b.rearrange("(p o) -> p o", o=1)).then_inc(weights_landed, 16)
            act.dma_start(tb_sb[:], theta_b.rearrange("(p o) -> p o", o=1)).then_inc(weights_landed, 16)
            act.dma_start(bn[:], bn_params).then_inc(weights_landed, 16)
            act.wait_ge(weights_landed, 16 * WEIGHT_DMAS)
            for li, s in enumerate(POOLS):
                last = nc.scalar.mul(gw_level[:, li, :, :], gw_sb[:], float(s) / T)
            last.then_inc(consts_ready, 1)
            act.wait_ge(ident_made, 1)
            nc.scalar.copy(ident_r[:], ident[:]).then_inc(consts_ready, 1)

            def save_phi_hi(b, parity):
                act.wait_ge(g_ready, b + 1)
                nc.scalar.activation(phi_hi[:, parity, COARSE:S], g_ps[:, 0, 0:FINE], ACT.Identity,
                                     bias=gb_sb[:, 0:1]).then_inc(phi_hi_ready, 1)
                nc.scalar.activation(phi_hi[:, parity, 0:COARSE], g_ps[:, 1, 0:COARSE], ACT.Identity,
                                     bias=gb_sb[:, 0:1]).then_inc(phi_hi_ready, 1)

            def save_gT(b, parity):
                act.wait_ge(gT_ready, b + 1)
                nc.scalar.copy(gT[0:SR, parity, :].rearrange("p (a n) -> p a n", a=2),
                               f_ps[0:SR, 0:2, 0:TPB * P]).then_inc(gT_saved, 1)

            def save_theta_hi(b, pair):
                act.wait_ge(theta_ready, 2 * b + pair + 1)
                nc.scalar.activation(theta_hi[:, chunk(2 * pair, 2)].rearrange("p (c n) -> p c n", c=2),
                                     theta_ps[pair][:, :, 0:CW], ACT.Identity,
                                     bias=tb_sb[:, 0:1]).then_inc(theta_hi_ready, 1)

            def exponentials(b, t, parity):
                act.wait_ge(max_ready, ST * b + t + 1)
                for half in range(2):
                    nc.scalar.activation(
                        probs[0:SR, parity, t, chunk(2 * half, 2)].rearrange("p (c n) -> p c n", c=2),
                        f_ps[0:SR, 2 * half:2 * half + 2, 0:CW], ACT.Exp, bias=neg_max[0:SR, t:t + 1],
                        accum_out=zhalf[0:SR, half, t:t + 1]).then_inc(probs_ready, 1)

            def group_hi(b, g, parity):
                if g < SLOTS:
                    act.wait_ge(probs_ready, 2 * ST * (b + 1))
                else:
                    act.wait_ge(group_used, GROUPS * b + g - SLOTS + 1)
                nc.scalar.copy(probs_hi[0:SR, g % SLOTS], group_of(g, parity)).then_inc(group_hi_ready, 1)

            def y_exponentials(b):
                act.wait_ge(ymax_ready, b + 1)
                nc.scalar.activation(y_sb[:], y_sb[:], ACT.Exp, bias=yneg_max[:, 0:1],
                                     accum_out=yzsum[:, 0:1]).then_inc(yexp_ready, 1)

            def relu(b, k):
                h, pair = k // 2, k % 2
                act.wait_ge(res_added, 4 * b + k + 1)
                cols = x_half(b, h)[:, chunk(2 * pair, 2)]
                nc.scalar.activation(cols, cols, ACT.Relu, bias=bn_c[:, h:h + 1],
                                     scale=bn_a[:, h:h + 1]).then_inc(relu_done, 1)

            def later_groups(b, c, parity):
                for g in range(SLOTS + GC * c, min(SLOTS + GC * (c + 1), GROUPS)):
                    group_hi(b, g, parity)

            def phase(p, parity, with_last=True, with_next=True):
                for t in range(ST):
                    if t == ST - 1 and with_next:
                        act.wait_ge(f_ready, 2 * ST * (p + 1))
                        save_theta_hi(p + 1, 0)
                    exponentials(p, t, parity)
                    if with_last and t < NC:
                        later_groups(p - 1, t, 1 - parity)
                    if with_last and t == NC:
                        y_exponentials(p - 1)
                    if with_next and t == ST - 2:
                        save_phi_hi(p + 1, 1 - parity)
                if with_next:
                    save_theta_hi(p + 1, 1)
                group_hi(p, 0, parity)
                group_hi(p, 1, parity)
                if with_last:
                    relu(p - 1, 0)
                if with_next:
                    save_gT(p + 1, 1 - parity)
                group_hi(p, 2, parity)
                if with_last:
                    relu(p - 1, 1)
                group_hi(p, 3, parity)
                if with_last:
                    relu(p - 1, 2)
                    relu(p - 1, 3)

            act.wait_ge(pads_cleared, 2)
            save_theta_hi(0, 0)
            save_phi_hi(0, 0)
            save_theta_hi(0, 1)
            save_gT(0, 0)
            phase(0, 0, with_last=False)
            act.wait_ge(consts_ready, 3)
            with act.Fori(1, LAST, 2) as p:
                phase(p, 1)
                phase(p + 1, 0)
            phase(LAST, LAST % 2, with_next=False)
            for c in range(NC):
                later_groups(LAST, c, LAST % 2)
            y_exponentials(LAST)
            for k in range(4):
                relu(LAST, k)

        @block.vector
        def _(dve):
            if SP > S:
                nc.vector.memset(phi_hi[:, :, S:SP].bitcast(F32), 0.0).then_inc(pads_cleared, 1)
                nc.vector.memset(phi_lo[:, :, S:SP].bitcast(F32), 0.0).then_inc(pads_cleared, 1)
            dve.wait_ge(weights_landed, 16 * WEIGHT_DMAS)
            nc.vector.tensor_scalar(bn_inv[:], bn[:, 4, :], BN_EPS, None, ALU.add).then_inc(bn_step, 1)
            dve.wait_ge(bn_step, 2)
            nc.vector.tensor_tensor(bn_a[:], bn_inv[:], bn[:, 1, :], ALU.mult).then_inc(bn_step, 1)
            nc.vector.tensor_tensor(bn_c[:], bn[:, 0, :], bn[:, 3, :], ALU.subtract).then_inc(bn_step, 1)
            dve.wait_ge(bn_step, 4)
            nc.vector.tensor_tensor(bn_c[:], bn_c[:], bn_a[:], ALU.mult).then_inc(bn_step, 1)
            dve.wait_ge(bn_step, 5)
            nc.vector.tensor_tensor(bn_c[:], bn_c[:], bn[:, 2, :], ALU.add).then_inc(consts_ready, 1)

            def low_part(dst, psum, bias, hi):
                return nc.vector.scalar_tensor_tensor(out=dst, in0=psum, scalar=bias, in1=hi,
                                                      op0=ALU.add, op1=ALU.subtract)

            def save_phi_lo(b, parity):
                dve.wait_ge(phi_hi_ready, 2 * b + 1)
                low_part(phi_lo[:, parity, COARSE:S], g_ps[:, 0, 0:FINE], gb_sb[:, 0:1],
                         phi_hi[:, parity, COARSE:S].bitcast(F32))
                dve.wait_ge(phi_hi_ready, 2 * b + 2)
                low_part(phi_lo[:, parity, 0:COARSE], g_ps[:, 1, 0:COARSE], gb_sb[:, 0:1],
                         phi_hi[:, parity, 0:COARSE].bitcast(F32)).then_inc(phi_lo_ready, 1)

            def save_theta_lo(b, pair):
                dve.wait_ge(theta_hi_ready, 2 * b + pair + 1)
                low_part(theta_lo[:, chunk(2 * pair, 2)].rearrange("p (c n) -> p c n", c=2),
                         theta_ps[pair][:, :, 0:CW], tb_sb[:, 0:1],
                         theta_hi[:, chunk(2 * pair, 2)].bitcast(F32).rearrange("p (c n) -> p c n", c=2)
                         ).then_inc(theta_lo_ready, 1)

            def maxima(b, t):
                for half in range(2):
                    dve.wait_ge(f_ready, 2 * (ST * b + t) + half + 1)
                    nc.vector.tensor_reduce(half_max[0:SR, half:half + 1],
                                            f_ps[0:SR, 2 * half:2 * half + 2, 0:CW], AX.XY, ALU.max,
                                            negate=True).then_inc(halves_ready, 1)
                dve.wait_ge(halves_ready, 2 * (ST * b + t + 1))
                nc.vector.tensor_tensor(neg_max[0:SR, t:t + 1], half_max[0:SR, 0:1], half_max[0:SR, 1:2],
                                        ALU.min).then_inc(max_ready, 1)

            def save_y(b, c):
                dve.wait_ge(group_used, GROUPS * b + GC * (c + 1))
                nc.vector.tensor_scalar(y_sb[:, chunk(c)], pair_a[:, c % 2, 0:CW], 1.0, None, ALU.mult,
                                        ALU.max, accum_out=ychunk_max[:, c:c + 1]).then_inc(y_saved, 1)

            def y_maximum(b):
                dve.wait_ge(y_saved, 4 * b + 4)
                nc.vector.tensor_reduce(yneg_max[:, 0:1], ychunk_max[:], AX.X, ALU.max,
                                        negate=True).then_inc(ymax_ready, 1)

            def scale_W(b):
                dve.wait_ge(yexp_ready, b + 1)
                nc.vector.reciprocal(yzinv[:, 0:1], yzsum[:, 0:1]).then_inc(yzinv_ready, 1)
                dve.wait_ge(yzinv_ready, b + 1)
                nc.vector.tensor_scalar(Ww_scaled[:], Ww_sb[:], yzinv[:, 0:1], None,
                                        ALU.mult).then_inc(W_scaled_ready, 1)

            def scale_gT(b, parity, lot):
                tiles = range(EARLY) if lot == 0 else range(EARLY, ST)
                dve.wait_ge(probs_ready, 2 * (ST * b + tiles[-1] + 1))
                span = slice(tiles[0], tiles[-1] + 1)
                nc.vector.tensor_tensor(zsum[0:SR, span], zhalf[0:SR, 0, span], zhalf[0:SR, 1, span],
                                        ALU.add).then_inc(zsum_ready, 1)
                dve.wait_ge(zsum_ready, 2 * b + lot + 1)
                nc.vector.reciprocal(zinv[0:SR, span], zsum[0:SR, span]).then_inc(zinv_ready, 1)
                dve.wait_ge(gT_saved, b + 1)
                dve.wait_ge(zinv_ready, 2 * b + lot + 1)
                for t in tiles:
                    cols = slice(t * P, (t + 1) * P)
                    last = nc.vector.tensor_scalar(gT_hi[0:SR, cols], gT[0:SR, parity, cols],
                                                   zinv[0:SR, t:t + 1], None, ALU.mult)
                last.then_inc(gT_hi_step, 1)
                dve.wait_ge(gT_hi_step, 2 * b + lot + 1)
                for t in tiles:
                    cols = slice(t * P, (t + 1) * P)
                    last = nc.vector.scalar_tensor_tensor(out=gT_lo[0:SR, cols], in0=gT[0:SR, parity, cols],
                                                          scalar=zinv[0:SR, t:t + 1],
                                                          in1=gT_hi[0:SR, cols].bitcast(F32),
                                                          op0=ALU.mult, op1=ALU.subtract)
                if lot == 1:
                    last.then_inc(gT_parts_ready, 1)

            def residual(b, k):
                h, pair = k // 2, k % 2
                dve.wait_ge(o_ready, 4 * b + k + 1)
                cols = x_half(b, h)[:, chunk(2 * pair, 2)].rearrange("p (c n) -> p c n", c=2)
                nc.vector.tensor_tensor(cols, out_ps[k][:, :, 0:CW], cols, ALU.add).then_inc(res_added, 1)

            def group_lo(b, g, parity):
                dve.wait_ge(group_hi_ready, GROUPS * b + g + 1)
                nc.vector.tensor_tensor(probs_lo[0:SR, g % SLOTS], group_of(g, parity),
                                        probs_hi[0:SR, g % SLOTS].bitcast(F32),
                                        ALU.subtract).then_inc(group_lo_ready_dve, 1)

            def pair_upper(b, parity, turn):
                dve.wait_ge(x_landed[parity][1], 16 * turn)
                if type(b) is not int or b > 0:
                    dve.wait_ge(pooled_ready, b)
                src = x_half(b, 1)
                nc.vector.tensor_tensor(pair_sums[:, 1, :], src[:, 0::2], src[:, 1::2],
                                        ALU.add).then_inc(pair_upper_ready, 1)

            def phase(p, parity, turn=0, with_last=True, with_next=True):
                for t in range(ST):
                    if with_last and 1 <= t <= len(DVE_GROUPS):
                        group_lo(p - 1, DVE_GROUPS[t - 1], 1 - parity)
                    maxima(p, t)
                    if with_last and 1 <= t <= NC:
                        save_y(p - 1, t - 1)
                    if with_next and t == 2:
                        pair_upper(p + 1, 1 - parity, turn)
                    if with_last and t == NC:
                        y_maximum(p - 1)
                    if t == NC:
                        scale_gT(p, parity, 0)
                        if with_last:
                            scale_W(p - 1)
                        if with_next:
                            save_phi_lo(p + 1, 1 - parity)
                if with_next:
                    save_theta_lo(p + 1, 0)
                    save_theta_lo(p + 1, 1)
                if with_last:
                    residual(p - 1, 0)
                scale_gT(p, parity, 1)
                if with_last:
                    residual(p - 1, 1)
                    residual(p - 1, 2)
                    residual(p - 1, 3)

            pair_upper(0, 0, 1)
            save_theta_lo(0, 0)
            save_phi_lo(0, 0)
            save_theta_lo(0, 1)
            phase(0, 0, 1, with_last=False)
            with dve.Fori(1, LAST, 2) as p:
                phase(p, 1, (p + 1) // 2 + 1)
                phase(p + 1, 0, (p + 1) // 2 + 1)
            phase(LAST, LAST % 2, with_next=False)
            for c in range(NC):
                if c < len(DVE_GROUPS):
                    group_lo(LAST, DVE_GROUPS[c], LAST % 2)
                save_y(LAST, c)
            y_maximum(LAST)
            scale_W(LAST)
            for k in range(4):
                residual(LAST, k)


_BN_PARAMS = ("W_b", "bn_gamma", "bn_beta", "bn_mean", "bn_var")


def kernel(**inputs):
    import numpy as _np
    import concourse.bacc as _bacc
    from concourse import mybir as _mybir
    from concourse.bass_utils import run_bass_kernel_spmd as _run

    nc = _bacc.Bacc("TRN2", target_bir_lowering=False, num_devices=1)
    arrays = {"x": _np.ascontiguousarray(inputs["x"])}
    for name in ("g_w", "theta_w", "W_w"):
        arrays[name + "T"] = _np.ascontiguousarray(_np.asarray(inputs["L0_conv_" + name]).T)
    for name in ("g_b", "theta_b"):
        arrays[name] = _np.ascontiguousarray(inputs["L0_conv_" + name])
    stacked = _np.stack([_np.asarray(inputs["L0_conv_" + name]) for name in _BN_PARAMS])
    arrays["bn_params"] = _np.ascontiguousarray(stacked.reshape(len(_BN_PARAMS), -1, P).transpose(2, 0, 1))
    aps = {n: nc.dram_tensor("in_" + n, a.shape, _mybir.dt.from_np(a.dtype), kind="ExternalInput").ap()
           for n, a in arrays.items()}
    out = nc.dram_tensor("out", arrays["x"].shape, _mybir.dt.float32, kind="ExternalOutput").ap()
    psp_nonlocal_kernel(nc, aps["x"], aps["g_wT"], aps["g_b"], aps["theta_wT"], aps["theta_b"], aps["W_wT"],
                        aps["bn_params"], out)
    r = _run(nc, [{"in_" + n: a for n, a in arrays.items()}], core_ids=[0])
    return r.results[0]["out"]
```

```python
from contextlib import ExitStack

import concourse.bass as bass
from concourse import mybir

F32 = mybir.dt.float32
F32R = mybir.dt.float32r
ALU = mybir.AluOpType
ACT = mybir.ActivationFunctionType
AX = mybir.AxisListType

P = 128
POOLS = (1, 4, 8, 16)
BN_EPS = 1e-5
XHALVES = 7


def psp_nonlocal_kernel(nc, x, g_wT, g_b, theta_wT, theta_b, W_wT, bn_params, out):
    B, C, T, V = x.shape
    C2 = g_wT.shape[1]
    N = T * V
    CH = C // P
    assert C == CH * P and C2 == P and CH == 2
    NC = 4
    CW = N // NC
    S = V * sum(POOLS)
    ST = -(-S // P)
    SR = -(-S // ST)
    SP = ST * SR
    GT = 2
    GC = ST // GT
    GROUPS = NC * GC
    SLOTS = 4
    DVE_GROUPS = (4, 7, 10)
    EARLY = 4
    BANK = 512
    assert CW <= BANK and N == NC * CW and ST == GC * GT and GROUPS % SLOTS == 0

    level_at, at = {}, 0
    for s in POOLS:
        level_at[s] = (at, at + V * s)
        at += V * s
    COARSE = level_at[POOLS[-1]][0]
    FINE = V * POOLS[-1]
    WINDOW = T // POOLS[-1]
    assert WINDOW == 4
    PYRAMID = [FINE >> i for i in range(1, POOLS[-1].bit_length())]

    ctx = ExitStack()
    with ctx:
        def sb(name, shape, dt=F32):
            return ctx.enter_context(nc.sbuf_tensor(name, shape, dt))

        def sem(name):
            return ctx.enter_context(nc.semaphore(name))

        x_ring = sb("x_ring", [P, XHALVES, N])
        pair_sums = sb("pair_sums", [P, CH, N // 2])
        quad_sums = sb("quad_sums", [P, CH, FINE])
        phi = sb("phi", [P, SP])
        phi_sums, sums_8 = quad_sums[:, 0, 0:COARSE], quad_sums[:, 1, 0:PYRAMID[2]]
        mean_scale = sb("mean_scale", [P, COARSE])
        phi_hi = sb("phi_hi", [P, 2, SP], F32R)
        phi_lo = sb("phi_lo", [P, 2, SP], F32R)
        theta_hi = sb("theta_hi", [P, N], F32R)
        theta_lo = sb("theta_lo", [P, N], F32R)
        gT = sb("gT", [P, 2, ST * P])
        gT_hi = sb("gT_hi", [P, ST * P], F32R)
        gT_lo = sb("gT_lo", [P, ST * P], F32R)
        probs = sb("probs", [P, 2, ST, N])
        probs_hi = sb("probs_hi", [P, SLOTS, GT, CW], F32R)
        probs_lo = sb("probs_lo", [P, SLOTS, GT, CW], F32R)
        neg_max = sb("neg_max", [P, ST])
        half_max = sb("half_max", [P, 2])
        zhalf = sb("zhalf", [P, 2, ST])
        zsum = sb("zsum", [P, ST])
        zinv = sb("zinv", [P, ST])
        y_sb = sb("y_sb", [P, N])
        ychunk_max = sb("ychunk_max", [P, NC])
        yneg_max = sb("yneg_max", [P, 1])
        yzsum = sb("yzsum", [P, 1])
        yzinv = sb("yzinv", [P, 1])
        gw_hi = sb("gw_hi", [P, CH, C2], F32R)
        gw_lo = sb("gw_lo", [P, CH, C2], F32R)
        gw_landing = y_sb[:, 0:CH * C2].rearrange("p (h o) -> p h o", h=CH)
        tw_sb = sb("tw_sb", [P, CH, C2])
        Ww_sb = sb("Ww_sb", [P, C])
        Ww_hi = sb("Ww_hi", [P, C], F32R)
        Ww_lo = sb("Ww_lo", [P, C], F32R)
        gb_sb = sb("gb_sb", [P, 1])
        tb_sb = sb("tb_sb", [P, 1])
        bn = sb("bn", [P, 5, CH])
        bn_exp = sb("bn_exp", [P, CH])
        bn_inv = sb("bn_inv", [P, CH])
        bn_a = sb("bn_a", [P, CH])
        bn_c = sb("bn_c", [P, CH])
        ident = sb("ident", [P, P])

        f_ps = ctx.enter_context(nc.psum_tensor("f_ps", [P, NC, BANK], F32))
        pair_a = ctx.enter_context(nc.psum_tensor("pair_a", [P, 2, BANK], F32))
        pair_b = ctx.enter_context(nc.psum_tensor("pair_b", [P, 2, BANK], F32))
        f_front, f_back = f_ps[:, 0:2, :], f_ps[:, 2:4, :]
        theta_ps = (pair_b, pair_a)
        g_ps = pair_a
        y_ps = pair_b
        out_ps = (pair_b, f_front, pair_b, pair_a)
        TPB = ST // 2
        assert ST % 2 == 0 and TPB * P <= BANK and FINE <= BANK and COARSE <= BANK

        x_landed = [[sem(f"x_landed_{parity}_{h}") for h in range(CH)] for parity in ("even", "odd")]
        weights_landed = sem("weights_landed")
        ident_made = sem("ident_made")
        bn_step = sem("bn_step")
        consts_ready = sem("consts_ready")
        pads_cleared = sem("pads_cleared")
        pool_step = sem("pool_step")
        pair_upper_ready = sem("pair_upper_ready")
        quads_ready = sem("quads_ready")
        phi_fine_ready = sem("phi_fine_ready")
        phi_ready = sem("phi_ready")
        gw_hi_ready = sem("gw_hi_ready")
        quads_hi_ready = sem("quads_hi_ready")
        quads_lo_ready = sem("quads_lo_ready")
        g_ready = sem("g_ready")
        phi_hi_ready = sem("phi_hi_ready")
        phi_lo_ready = sem("phi_lo_ready")
        gT_ready = sem("gT_ready")
        gT_saved = sem("gT_saved")
        theta_ready = sem("theta_ready")
        theta_hi_ready = sem("theta_hi_ready")
        theta_lo_ready = sem("theta_lo_ready")
        f_ready = sem("f_ready")
        halves_ready = sem("halves_ready")
        max_ready = sem("max_ready")
        probs_ready = sem("probs_ready")
        zsum_ready = sem("zsum_ready")
        zinv_ready = sem("zinv_ready")
        gT_hi_step = sem("gT_hi_step")
        gT_parts_ready = sem("gT_parts_ready")
        group_hi_ready = sem("group_hi_ready")
        group_lo_ready = sem("group_lo_ready")
        group_lo_ready_dve = sem("group_lo_ready_dve")
        group_used = sem("group_used")
        y_saved = sem("y_saved")
        ymax_ready = sem("ymax_ready")
        yexp_ready = sem("yexp_ready")
        yzinv_ready = sem("yzinv_ready")
        y_hi_ready = sem("y_hi_ready")
        y_lo_ready = sem("y_lo_ready")
        W_hi_ready = sem("W_hi_ready")
        W_parts_ready = sem("W_parts_ready")
        o_ready = sem("o_ready")
        res_added = sem("res_added")
        relu_done = sem("relu_done")
        stored = [[sem(f"stored_{half}_{pair}") for pair in range(2)] for half in ("lower", "upper")]

        x_dram = x.rearrange("b (h p) t v -> b p h (t v)", p=P)
        out_dram = out.rearrange("b (h p) t v -> b h p (t v)", p=P)

        def x_half(b, h):
            return x_ring[:, bass.ds((CH * b + h) % XHALVES, 1), :].rearrange("p o n -> p (o n)")

        def chunk(c, n=1):
            return slice(c * CW, (c + n) * CW)

        def tile(t):
            return slice(t * SR, (t + 1) * SR)

        def group_of(g, parity):
            t = GT * (g % GC)
            return probs[0:SR, parity, t:t + GT, chunk(g // GC)]

        Y_SLOT = [SLOTS - 2, SLOTS - 1]
        assert GT == 2
        Q_SLOT = 0
        assert GT == CH and FINE == CW
        WEIGHT_DMAS = 6
        LANDED = 2 * 16
        LAST = B - 1
        block = ctx.enter_context(nc.Block())

        @block.sync
        def _(sp):
            BACK = [-(-(XHALVES - h) // CH) for h in range(CH)]
            FREES = [(h - XHALVES) % CH for h in range(CH)]

            def load_x(b, h, parity):
                for pair in range(2):
                    if type(b) is not int or b >= BACK[h]:
                        sp.wait_ge(stored[FREES[h]][pair], 16 * (b - BACK[h] + 1))
                    cols = chunk(2 * pair, 2)
                    sp.dma_start(x_half(b, h)[:, cols], x_dram[b, :, h, cols]).then_inc(x_landed[parity][h], 16)

            def store(b, h):
                for pair in range(2):
                    sp.wait_ge(relu_done, 4 * b + 2 * h + pair + 1)
                    cols = chunk(2 * pair, 2)
                    sp.dma_start(out_dram[b, h, :, cols], x_half(b, h)[:, cols]).then_inc(stored[h][pair], 16)

            for h in range(CH):
                load_x(0, h, 0)
            sp.wait_ge(weights_landed, 16 * WEIGHT_DMAS)
            for h in range(CH):
                load_x(1, h, 1)
            for h in range(CH):
                sp.wait_ge(x_landed[0][h], LANDED)
                load_x(2, h, 0)
            sp.wait_ge(x_landed[1][0], LANDED)
            load_x(3, 0, 1)

            def store_and_load(p, parity):
                store(p - 1, 0)
                load_x(p + 2, 1, parity)
                store(p - 1, 1)
                load_x(p + 3, 0, 1 - parity)

            with sp.Fori(1, LAST - 3, 2) as p:
                store_and_load(p, 1)
                store_and_load(p + 1, 0)
            store(LAST - 3, 0)
            load_x(LAST, 1, LAST % 2)
            store(LAST - 3, 1)
            for b in (LAST - 2, LAST - 1, LAST):
                for h in range(CH):
                    store(b, h)
            for h in range(CH):
                for pair in range(2):
                    sp.wait_ge(stored[h][pair], 16 * B)

        @block.gpsimd
        def _(pool):
            nc.gpsimd.memset(ident[:], 0.0).then_inc(pool_step, 1)
            nc.gpsimd.memset(bn_exp[:], -0.5).then_inc(pool_step, 1)
            for s in POOLS[:-1]:
                last = nc.gpsimd.memset(mean_scale[:, level_at[s][0]:level_at[s][1]], float(s) / POOLS[-1])
            last.then_inc(pool_step, 1)
            pool.wait_ge(pool_step, 3)
            nc.gpsimd.affine_select(out=ident[:], in_=ident[:], compare_op=ALU.not_equal, fill=1.0, base=0,
                                    pattern=[[-1, P]], channel_multiplier=1).then_inc(ident_made, 1)
            SETUP_STEPS = 3
            HALVINGS = len(PYRAMID)
            STEPS = 1 + HALVINGS

            def pair_lower(b, parity, turn, part):
                if part == 0:
                    pool.wait_ge(x_landed[parity][0], LANDED * turn)
                    if type(b) is not int or b > 0:
                        pool.wait_ge(quads_ready, b)
                src = x_half(b, 0)[:, part * N // 2:(part + 1) * N // 2]
                last = nc.gpsimd.tensor_tensor(pair_sums[:, 0, part * N // 4:(part + 1) * N // 4],
                                               src[:, 0::2], src[:, 1::2], ALU.add)
                if part == 1:
                    last.then_inc(pool_step, 1)

            def quads(b):
                if type(b) is not int or b > 0:
                    pool.wait_ge(g_ready, b)
                    pool.wait_ge(phi_ready, b)
                pool.wait_ge(pool_step, SETUP_STEPS + STEPS * b + 1)
                pool.wait_ge(pair_upper_ready, b + 1)
                nc.gpsimd.tensor_tensor(quad_sums[:], pair_sums[:, :, 0::2], pair_sums[:, :, 1::2],
                                        ALU.add).then_inc(quads_ready, 1)

            def coarse_phi(b):
                pool.wait_ge(phi_fine_ready, b + 1)

                def sums(s):
                    return phi_sums[:, level_at[s][0]:level_at[s][1]]

                src = phi[:, COARSE:S]
                for i, dst in enumerate((sums(8), sums(4), sums_8, sums(1))):
                    if i > 0:
                        pool.wait_ge(pool_step, SETUP_STEPS + STEPS * b + i + 1)
                    nc.gpsimd.tensor_tensor(dst, src[:, 0::2], src[:, 1::2], ALU.add).then_inc(pool_step, 1)
                    src = dst
                pool.wait_ge(pool_step, SETUP_STEPS + STEPS * (b + 1))
                nc.gpsimd.tensor_tensor(phi[:, 0:COARSE], phi_sums, mean_scale[:],
                                        ALU.mult).then_inc(phi_ready, 1)

            def save_phi_lo(b, parity):
                pool.wait_ge(phi_hi_ready, b + 1)
                nc.gpsimd.tensor_tensor(phi_lo[:, parity, :], phi[:], phi_hi[:, parity, :].bitcast(F32),
                                        ALU.subtract).then_inc(phi_lo_ready, 1)

            def group_lo(b, g, parity):
                if g in DVE_GROUPS:
                    return
                pool.wait_ge(group_hi_ready, GROUPS * b + g + 1)
                nc.gpsimd.tensor_tensor(probs_lo[0:SR, g % SLOTS], group_of(g, parity),
                                        probs_hi[0:SR, g % SLOTS].bitcast(F32),
                                        ALU.subtract).then_inc(group_lo_ready, 1)

            def phase(p, parity, turn, with_last=True, with_next=True):
                for g in range(SLOTS, GROUPS):
                    if with_next and g in (5, 8):
                        pair_lower(p + 1, 1 - parity, turn, (5, 8).index(g))
                    if with_last:
                        group_lo(p - 1, g, 1 - parity)
                if with_next:
                    quads(p + 1)
                    coarse_phi(p + 1)
                    save_phi_lo(p + 1, 1 - parity)
                for g in range(SLOTS):
                    group_lo(p, g, parity)

            for part in range(2):
                pair_lower(0, 0, 1, part)
            quads(0)
            pool.wait_ge(bn_step, 1)
            nc.gpsimd.tensor_tensor(bn_inv[:], bn_inv[:], bn_exp[:], ALU.pow).then_inc(bn_step, 1)
            coarse_phi(0)
            save_phi_lo(0, 0)
            phase(0, 0, 1, with_last=False)
            with pool.Fori(1, LAST, 2) as p:
                phase(p, 1, (p + 1) // 2 + 1)
                phase(p + 1, 0, (p + 1) // 2 + 1)
            phase(LAST, LAST % 2, 0, with_next=False)
            for g in range(SLOTS, GROUPS):
                group_lo(LAST, g, LAST % 2)

        @block.tensor
        def _(pe):
            def make_g(b):
                pe.wait_ge(quads_hi_ready, b + 1)
                pe.wait_ge(quads_lo_ready, b + 1)
                dst = g_ps[:, 0, 0:FINE]
                for h in range(CH):
                    x_hi, x_lo = probs_hi[:, Q_SLOT, h, 0:FINE], probs_lo[:, Q_SLOT, h, 0:FINE]
                    nc.tensor.matmul(dst, gw_hi[:, h, :], x_hi, start=(h == 0), stop=False)
                    nc.tensor.matmul(dst, gw_lo[:, h, :], x_hi, start=False, stop=False)
                    mm = nc.tensor.matmul(dst, gw_hi[:, h, :], x_lo, start=False, stop=(h == CH - 1))
                mm.then_inc(g_ready, 1)

            def transpose_phi(b):
                pe.wait_ge(phi_ready, b + 1)
                for t in range(ST):
                    dst = f_back[0:SR, t // TPB, (t % TPB) * P:(t % TPB + 1) * P]
                    mm = nc.tensor.transpose(dst, phi[:, tile(t)], ident[:])
                mm.then_inc(gT_ready, 1)

            def make_theta(b, pair):
                for c in range(2):
                    for h in range(CH):
                        cols = x_half(b, h)[:, chunk(2 * pair + c)]
                        mm = nc.tensor.matmul(theta_ps[pair][:, c, 0:CW], tw_sb[:, h, :], cols,
                                              start=(h == 0), stop=(h == CH - 1))
                mm.then_inc(theta_ready, 1)

            def scores(b, t, parity):
                for c in range(NC):
                    if t > 0 and c % 2 == 0:
                        pe.wait_ge(probs_ready, 2 * (ST * b + t - 1) + c // 2 + 1)
                    if t == 0 and c == 0 and (type(b) is not int or b > 1):
                        pe.wait_ge(res_added, 4 * (b - 2) + 2)
                    if t == 0 and c == 0:
                        pe.wait_ge(phi_hi_ready, b + 1)
                        pe.wait_ge(phi_lo_ready, b + 1)
                    if t == 0 and c == 2:
                        pe.wait_ge(gT_saved, b + 1)
                    if t == 0 and c % 2 == 0:
                        pe.wait_ge(theta_hi_ready, 2 * b + c // 2 + 1)
                        pe.wait_ge(theta_lo_ready, 2 * b + c // 2 + 1)
                    dst = f_ps[0:SR, c, 0:CW]
                    hi, lo = phi_hi[:, parity, tile(t)], phi_lo[:, parity, tile(t)]
                    nc.tensor.matmul(dst, hi, theta_hi[:, chunk(c)], start=True, stop=False)
                    nc.tensor.matmul(dst, hi, theta_lo[:, chunk(c)], start=False, stop=False)
                    mm = nc.tensor.matmul(dst, lo, theta_hi[:, chunk(c)], start=False, stop=True)
                    if c % 2 == 1:
                        mm.then_inc(f_ready, 1)

            def make_y(b, c):
                if c == 0:
                    pe.wait_ge(gT_parts_ready, 2 * b + 1)
                    if type(b) is not int or b > 0:
                        pe.wait_ge(res_added, 4 * b - 1)
                if c >= 2:
                    pe.wait_ge(y_saved, 4 * b + c - 1)
                for q in range(GC):
                    g = GC * c + q
                    if c == 0 and GT * q == EARLY:
                        pe.wait_ge(gT_parts_ready, 2 * b + 2)
                    pe.wait_ge(group_hi_ready, GROUPS * b + g + 1)
                    if g in DVE_GROUPS:
                        pe.wait_ge(group_lo_ready_dve, len(DVE_GROUPS) * b + DVE_GROUPS.index(g) + 1)
                    else:
                        before = sum(q < g for q in range(GROUPS) if q not in DVE_GROUPS)
                        pe.wait_ge(group_lo_ready, (GROUPS - len(DVE_GROUPS)) * b + before + 1)
                    for i in range(GT):
                        t = GT * q + i
                        dst = y_ps[:, c % 2, 0:CW]
                        hi, lo = gT_hi[0:SR, t * P:(t + 1) * P], gT_lo[0:SR, t * P:(t + 1) * P]
                        p_hi, p_lo = probs_hi[0:SR, g % SLOTS, i], probs_lo[0:SR, g % SLOTS, i]
                        nc.tensor.matmul(dst, hi, p_hi, start=(t == 0), stop=False)
                        nc.tensor.matmul(dst, lo, p_hi, start=False, stop=False)
                        mm = nc.tensor.matmul(dst, hi, p_lo, start=False, stop=(t == ST - 1))
                    mm.then_inc(group_used, 1)

            def make_out(b, k):
                h, pair = k // 2, k % 2
                if k < 2:
                    pe.wait_ge(y_hi_ready, 2 * b + pair + 1)
                    pe.wait_ge(y_lo_ready, 2 * b + pair + 1)
                hi, lo = Ww_hi[:, h * P:(h + 1) * P], Ww_lo[:, h * P:(h + 1) * P]
                for c in range(2):
                    dst = out_ps[k][:, c, 0:CW]
                    y_hi, y_lo = probs_hi[:, Y_SLOT[pair], c], probs_lo[:, Y_SLOT[pair], c]
                    nc.tensor.matmul(dst, hi, y_hi, start=True, stop=False)
                    nc.tensor.matmul(dst, lo, y_hi, start=False, stop=False)
                    mm = nc.tensor.matmul(dst, hi, y_lo, start=False, stop=True)
                mm.then_inc(o_ready, 1)

            def end_of_phase(p, parity, with_last, with_next):
                if with_next:
                    pe.wait_ge(phi_fine_ready, p + 2)
                    make_theta(p + 1, 1)
                if with_last:
                    pe.wait_ge(W_parts_ready, p)
                    if with_next:
                        pe.wait_ge(theta_hi_ready, 2 * (p + 1) + 1)
                        pe.wait_ge(theta_lo_ready, 2 * (p + 1) + 1)
                    make_out(p - 1, 0)
                has_batch = type(p) is not int or 0 <= p < B
                if with_last:
                    if has_batch:
                        pe.wait_ge(probs_ready, 2 * ST * (p + 1) - 1)
                    make_out(p - 1, 1)
                if has_batch:
                    pe.wait_ge(probs_ready, 2 * ST * (p + 1))
                if with_next:
                    transpose_phi(p + 1)
                if with_last:
                    pe.wait_ge(res_added, 4 * (p - 1) + 1)
                    make_out(p - 1, 2)
                    if not with_next:
                        make_out(p - 1, 3)

            def has_previous(p):
                return type(p) is not int or p > 1

            def phase(p, parity, turn=0, with_last=True, with_next=True):
                for t in range(ST):
                    scores(p, t, parity)
                    if t == 0 and has_previous(p):
                        make_out(p - 2, 3)
                    if with_last and t < NC:
                        make_y(p - 1, t)
                    if with_next and t == (NC if with_last else 0):
                        for h in range(CH):
                            pe.wait_ge(x_landed[1 - parity][h], LANDED * turn)
                        if with_last:
                            pe.wait_ge(y_saved, 4 * p)
                        make_theta(p + 1, 0)
                    if with_next and t == NC:
                        if has_previous(p):
                            pe.wait_ge(res_added, 4 * (p - 1))
                        make_g(p + 1)
                end_of_phase(p, parity, with_last, with_next)

            pe.wait_ge(weights_landed, 16 * WEIGHT_DMAS)
            pe.wait_ge(ident_made, 1)
            if SP > S:
                pe.wait_ge(pads_cleared, 1)
            for h in range(CH):
                pe.wait_ge(x_landed[0][h], LANDED)
            make_theta(0, 0)
            pe.wait_ge(consts_ready, 1)
            make_g(0)
            end_of_phase(-1, 1, False, True)
            phase(0, 0, 1, with_last=False)
            phase(1, 1, 2)
            phase(2, 0, 2)
            with pe.Fori(3, LAST, 2) as p:
                phase(p, 1, (p + 1) // 2 + 1)
                phase(p + 1, 0, (p + 1) // 2 + 1)
            phase(LAST, LAST % 2, with_next=False)
            for c in range(NC):
                make_y(LAST, c)
            pe.wait_ge(y_saved, 4 * B)
            end_of_phase(B, 0, True, False)

        @block.scalar
        def _(act):
            act.dma_start(gw_landing, g_wT.rearrange("(h p) o -> p h o", p=P)).then_inc(weights_landed, 16)
            act.dma_start(tw_sb[:], theta_wT.rearrange("(h p) o -> p h o", p=P)).then_inc(weights_landed, 16)
            act.dma_start(Ww_sb[:], W_wT).then_inc(weights_landed, 16)
            act.dma_start(gb_sb[:], g_b.rearrange("(p o) -> p o", o=1)).then_inc(weights_landed, 16)
            act.dma_start(tb_sb[:], theta_b.rearrange("(p o) -> p o", o=1)).then_inc(weights_landed, 16)
            act.dma_start(bn[:], bn_params).then_inc(weights_landed, 16)
            act.wait_ge(weights_landed, 16 * WEIGHT_DMAS)
            nc.scalar.mul(gw_hi[:], gw_landing, 1.0 / WINDOW).then_inc(gw_hi_ready, 1)

            def quad_hi(b):
                act.wait_ge(quads_ready, b + 1)
                if type(b) is not int or b > 1:
                    act.wait_ge(group_used, GROUPS * (b - 2) + 2 * SLOTS + 1)
                nc.scalar.copy(probs_hi[:, Q_SLOT], quad_sums[:]).then_inc(quads_hi_ready, 1)

            def save_phi_fine(b):
                act.wait_ge(g_ready, b + 1)
                if type(b) is not int or b > 0:
                    act.wait_ge(phi_lo_ready, b)
                    act.wait_ge(gT_ready, b)
                nc.scalar.activation(phi[:, COARSE:S], g_ps[:, 0, 0:FINE], ACT.Identity,
                                     bias=gb_sb[:, 0:1]).then_inc(phi_fine_ready, 1)

            def save_phi_hi(b, parity):
                act.wait_ge(phi_ready, b + 1)
                nc.scalar.copy(phi_hi[:, parity, :], phi[:]).then_inc(phi_hi_ready, 1)

            def save_gT(b, parity):
                act.wait_ge(gT_ready, b + 1)
                nc.scalar.copy(gT[0:SR, parity, :].rearrange("p (a n) -> p a n", a=2),
                               f_back[0:SR, :, 0:TPB * P]).then_inc(gT_saved, 1)

            def save_theta_hi(b, pair):
                act.wait_ge(theta_ready, 2 * b + pair + 1)
                nc.scalar.activation(theta_hi[:, chunk(2 * pair, 2)].rearrange("p (c n) -> p c n", c=2),
                                     theta_ps[pair][:, :, 0:CW], ACT.Identity,
                                     bias=tb_sb[:, 0:1]).then_inc(theta_hi_ready, 1)

            def exponentials(b, t, parity):
                act.wait_ge(max_ready, ST * b + t + 1)
                for half in range(2):
                    nc.scalar.activation(
                        probs[0:SR, parity, t, chunk(2 * half, 2)].rearrange("p (c n) -> p c n", c=2),
                        f_ps[0:SR, 2 * half:2 * half + 2, 0:CW], ACT.Exp, bias=neg_max[0:SR, t:t + 1],
                        accum_out=zhalf[0:SR, half, t:t + 1]).then_inc(probs_ready, 1)

            def group_hi(b, g, parity):
                if g < SLOTS:
                    act.wait_ge(probs_ready, 2 * ST * (b + 1))
                    if g in Y_SLOT and (type(b) is not int or b > 0):
                        act.wait_ge(o_ready, 4 * (b - 1) + 3 + Y_SLOT.index(g))
                else:
                    act.wait_ge(group_used, GROUPS * b + g - SLOTS + 1)
                nc.scalar.copy(probs_hi[0:SR, g % SLOTS], group_of(g, parity)).then_inc(group_hi_ready, 1)

            def y_exponentials(b):
                act.wait_ge(ymax_ready, b + 1)
                nc.scalar.activation(y_sb[:], y_sb[:], ACT.Exp, bias=yneg_max[:, 0:1],
                                     accum_out=yzsum[:, 0:1]).then_inc(yexp_ready, 1)

            def y_hi(b, pair):
                act.wait_ge(yexp_ready, b + 1)
                nc.scalar.copy(probs_hi[:, Y_SLOT[pair]],
                               y_sb[:, chunk(2 * pair, 2)].rearrange("p (c n) -> p c n", c=2)
                               ).then_inc(y_hi_ready, 1)

            def relu(b, k):
                h, pair = k // 2, k % 2
                act.wait_ge(res_added, 4 * b + k + 1)
                cols = x_half(b, h)[:, chunk(2 * pair, 2)]
                nc.scalar.activation(cols, cols, ACT.Relu, bias=bn_c[:, h:h + 1],
                                     scale=bn_a[:, h:h + 1]).then_inc(relu_done, 1)

            def groups_hi(b, groups, parity):
                for g in groups:
                    group_hi(b, g, parity)

            def phase(p, parity, with_last=True, with_next=True):
                if with_last:
                    group_hi(p - 1, 10, 1 - parity)
                exponentials(p, 2, parity)
                if with_last:
                    groups_hi(p - 1, range(11, GROUPS), 1 - parity)
                exponentials(p, 3, parity)
                if with_next:
                    quad_hi(p + 1)
                if with_last:
                    y_exponentials(p - 1)
                    y_hi(p - 1, 0)
                exponentials(p, 4, parity)
                if with_next:
                    save_phi_fine(p + 1)
                if with_last:
                    y_hi(p - 1, 1)
                if with_next:
                    act.wait_ge(f_ready, 2 * ST * (p + 1))
                    save_theta_hi(p + 1, 0)
                    save_phi_hi(p + 1, 1 - parity)
                exponentials(p, 5, parity)
                group_hi(p, 0, parity)
                if with_next:
                    save_theta_hi(p + 1, 1)
                    save_gT(p + 1, 1 - parity)
                groups_hi(p, range(1, 3), parity)
                if with_last:
                    relu(p - 1, 0)
                    relu(p - 1, 1)
                groups_hi(p, range(3, 5), parity)
                if with_next:
                    exponentials(p + 1, 0, 1 - parity)
                group_hi(p, 5, parity)
                if with_last:
                    relu(p - 1, 2)
                groups_hi(p, range(6, 8), parity)
                if with_next:
                    exponentials(p + 1, 1, 1 - parity)
                groups_hi(p, range(8, 10), parity)
                if with_last:
                    relu(p - 1, 3)

            quad_hi(0)
            save_theta_hi(0, 0)
            save_phi_fine(0)
            save_theta_hi(0, 1)
            if SP > S:
                act.wait_ge(pads_cleared, 1)
            save_phi_hi(0, 0)
            save_gT(0, 0)
            exponentials(0, 0, 0)
            exponentials(0, 1, 0)
            phase(0, 0, with_last=False)
            act.wait_ge(consts_ready, 2)
            with act.Fori(1, LAST, 2) as p:
                phase(p, 1)
                phase(p + 1, 0)
            phase(LAST, LAST % 2, with_next=False)
            groups_hi(LAST, range(10, GROUPS), LAST % 2)
            y_exponentials(LAST)
            for pair in range(2):
                y_hi(LAST, pair)
            for k in range(4):
                relu(LAST, k)

        @block.vector
        def _(dve):
            if SP > S:
                nc.vector.memset(phi[:, S:SP], 0.0).then_inc(pads_cleared, 1)

            def low_part(dst, psum, bias, hi):
                return nc.vector.scalar_tensor_tensor(out=dst, in0=psum, scalar=bias, in1=hi,
                                                      op0=ALU.add, op1=ALU.subtract)

            def save_theta_lo(b, pair):
                dve.wait_ge(theta_hi_ready, 2 * b + pair + 1)
                low_part(theta_lo[:, chunk(2 * pair, 2)].rearrange("p (c n) -> p c n", c=2),
                         theta_ps[pair][:, :, 0:CW], tb_sb[:, 0:1],
                         theta_hi[:, chunk(2 * pair, 2)].bitcast(F32).rearrange("p (c n) -> p c n", c=2)
                         ).then_inc(theta_lo_ready, 1)

            def maxima(b, t):
                for half in range(2):
                    dve.wait_ge(f_ready, 2 * (ST * b + t) + half + 1)
                    nc.vector.tensor_reduce(half_max[0:SR, half:half + 1],
                                            f_ps[0:SR, 2 * half:2 * half + 2, 0:CW], AX.XY, ALU.max,
                                            negate=True).then_inc(halves_ready, 1)
                dve.wait_ge(halves_ready, 2 * (ST * b + t + 1))
                nc.vector.tensor_tensor(neg_max[0:SR, t:t + 1], half_max[0:SR, 0:1], half_max[0:SR, 1:2],
                                        ALU.min).then_inc(max_ready, 1)

            def save_y(b, c):
                if c == 0 and (type(b) is not int or b > 0):
                    dve.wait_ge(y_lo_ready, 2 * b)
                dve.wait_ge(group_used, GROUPS * b + GC * (c + 1))
                nc.vector.tensor_scalar(y_sb[:, chunk(c)], y_ps[:, c % 2, 0:CW], 1.0, None, ALU.mult,
                                        ALU.max, accum_out=ychunk_max[:, c:c + 1]).then_inc(y_saved, 1)

            def y_maximum(b):
                dve.wait_ge(y_saved, 4 * b + 4)
                nc.vector.tensor_reduce(yneg_max[:, 0:1], ychunk_max[:], AX.X, ALU.max,
                                        negate=True).then_inc(ymax_ready, 1)

            def quad_lo(b):
                dve.wait_ge(quads_hi_ready, b + 1)
                nc.vector.tensor_tensor(probs_lo[:, Q_SLOT], quad_sums[:], probs_hi[:, Q_SLOT].bitcast(F32),
                                        ALU.subtract).then_inc(quads_lo_ready, 1)

            def invert_y_sum(b):
                dve.wait_ge(yexp_ready, b + 1)
                nc.vector.reciprocal(yzinv[:, 0:1], yzsum[:, 0:1]).then_inc(yzinv_ready, 1)

            def scale_W_hi(b):
                dve.wait_ge(yzinv_ready, b + 1)
                nc.vector.tensor_scalar(Ww_hi[:], Ww_sb[:], yzinv[:, 0:1], None,
                                        ALU.mult).then_inc(W_hi_ready, 1)

            def scale_W_lo(b):
                dve.wait_ge(W_hi_ready, b + 1)
                nc.vector.scalar_tensor_tensor(out=Ww_lo[:], in0=Ww_sb[:], scalar=yzinv[:, 0:1],
                                               in1=Ww_hi[:].bitcast(F32), op0=ALU.mult,
                                               op1=ALU.subtract).then_inc(W_parts_ready, 1)

            def y_lo(b, pair):
                dve.wait_ge(y_hi_ready, 2 * b + pair + 1)
                nc.vector.tensor_tensor(probs_lo[:, Y_SLOT[pair]],
                                        y_sb[:, chunk(2 * pair, 2)].rearrange("p (c n) -> p c n", c=2),
                                        probs_hi[:, Y_SLOT[pair]].bitcast(F32),
                                        ALU.subtract).then_inc(y_lo_ready, 1)

            LOTS = (range(EARLY), range(EARLY, ST))

            def sum_halves(b, lot):
                tiles = LOTS[lot]
                dve.wait_ge(probs_ready, 2 * (ST * b + tiles[-1] + 1))
                span = slice(tiles[0], tiles[-1] + 1)
                nc.vector.tensor_tensor(zsum[0:SR, span], zhalf[0:SR, 0, span], zhalf[0:SR, 1, span],
                                        ALU.add).then_inc(zsum_ready, 1)

            def invert_sums(b, lot):
                span = slice(LOTS[lot][0], LOTS[lot][-1] + 1)
                dve.wait_ge(zsum_ready, 2 * b + lot + 1)
                nc.vector.reciprocal(zinv[0:SR, span], zsum[0:SR, span]).then_inc(zinv_ready, 1)

            def scale_gT_hi(b, parity, lot):
                dve.wait_ge(gT_saved, b + 1)
                dve.wait_ge(zinv_ready, 2 * b + lot + 1)
                for t in LOTS[lot]:
                    cols = slice(t * P, (t + 1) * P)
                    last = nc.vector.tensor_scalar(gT_hi[0:SR, cols], gT[0:SR, parity, cols],
                                                   zinv[0:SR, t:t + 1], None, ALU.mult)
                last.then_inc(gT_hi_step, 1)

            def scale_gT_lo(b, parity, lot):
                dve.wait_ge(gT_hi_step, 2 * b + lot + 1)
                for t in LOTS[lot]:
                    cols = slice(t * P, (t + 1) * P)
                    last = nc.vector.scalar_tensor_tensor(out=gT_lo[0:SR, cols], in0=gT[0:SR, parity, cols],
                                                          scalar=zinv[0:SR, t:t + 1],
                                                          in1=gT_hi[0:SR, cols].bitcast(F32),
                                                          op0=ALU.mult, op1=ALU.subtract)
                last.then_inc(gT_parts_ready, 1)

            def residual(b, k):
                h, pair = k // 2, k % 2
                dve.wait_ge(o_ready, 4 * b + k + 1)
                cols = x_half(b, h)[:, chunk(2 * pair, 2)].rearrange("p (c n) -> p c n", c=2)
                nc.vector.tensor_tensor(cols, out_ps[k][:, :, 0:CW], cols, ALU.add).then_inc(res_added, 1)

            def group_lo(b, g, parity):
                dve.wait_ge(group_hi_ready, GROUPS * b + g + 1)
                nc.vector.tensor_tensor(probs_lo[0:SR, g % SLOTS], group_of(g, parity),
                                        probs_hi[0:SR, g % SLOTS].bitcast(F32),
                                        ALU.subtract).then_inc(group_lo_ready_dve, 1)

            def pair_upper(b, parity, turn):
                dve.wait_ge(x_landed[parity][1], LANDED * turn)
                if type(b) is not int or b > 0:
                    dve.wait_ge(quads_ready, b)
                src = x_half(b, 1)
                nc.vector.tensor_tensor(pair_sums[:, 1, :], src[:, 0::2], src[:, 1::2],
                                        ALU.add).then_inc(pair_upper_ready, 1)

            def phase(p, parity, turn=0, with_last=True, with_next=True):
                for t in range(1, ST):
                    if with_last and t == NC:
                        save_y(p - 1, NC - 1)
                        y_maximum(p - 1)
                    maxima(p, t)
                    if with_last and t < NC:
                        save_y(p - 1, t - 1)
                    if with_last and t < len(DVE_GROUPS):
                        group_lo(p - 1, DVE_GROUPS[t], 1 - parity)
                    if with_next and t == 2:
                        pair_upper(p + 1, 1 - parity, turn)
                    if t == NC:
                        if with_next:
                            quad_lo(p + 1)
                        sum_halves(p, 0)
                        if with_last:
                            invert_y_sum(p - 1)
                            y_lo(p - 1, 0)
                        invert_sums(p, 0)
                        if with_last:
                            scale_W_hi(p - 1)
                        scale_gT_hi(p, parity, 0)
                        if with_last:
                            scale_W_lo(p - 1)
                if with_next:
                    save_theta_lo(p + 1, 0)
                if with_last:
                    y_lo(p - 1, 1)
                scale_gT_lo(p, parity, 0)
                if with_last:
                    residual(p - 1, 0)
                sum_halves(p, 1)
                if with_last:
                    residual(p - 1, 1)
                if with_next:
                    save_theta_lo(p + 1, 1)
                invert_sums(p, 1)
                if with_last:
                    residual(p - 1, 2)
                scale_gT_hi(p, parity, 1)
                scale_gT_lo(p, parity, 1)
                if with_next:
                    maxima(p + 1, 0)
                if with_last:
                    residual(p - 1, 3)
                group_lo(p, DVE_GROUPS[0], parity)

            pair_upper(0, 0, 1)
            dve.wait_ge(weights_landed, 16 * WEIGHT_DMAS)
            nc.vector.tensor_scalar(bn_inv[:], bn[:, 4, :], BN_EPS, None, ALU.add).then_inc(bn_step, 1)
            dve.wait_ge(gw_hi_ready, 1)
            nc.vector.scalar_tensor_tensor(out=gw_lo[:], in0=gw_landing, scalar=1.0 / WINDOW,
                                           in1=gw_hi[:].bitcast(F32), op0=ALU.mult,
                                           op1=ALU.subtract).then_inc(consts_ready, 1)
            quad_lo(0)
            save_theta_lo(0, 0)
            save_theta_lo(0, 1)
            dve.wait_ge(bn_step, 2)
            nc.vector.tensor_tensor(bn_a[:], bn_inv[:], bn[:, 1, :], ALU.mult).then_inc(bn_step, 1)
            nc.vector.tensor_tensor(bn_c[:], bn[:, 0, :], bn[:, 3, :], ALU.subtract).then_inc(bn_step, 1)
            dve.wait_ge(bn_step, 4)
            nc.vector.tensor_tensor(bn_c[:], bn_c[:], bn_a[:], ALU.mult).then_inc(bn_step, 1)
            dve.wait_ge(bn_step, 5)
            nc.vector.tensor_tensor(bn_c[:], bn_c[:], bn[:, 2, :], ALU.add).then_inc(consts_ready, 1)
            maxima(0, 0)
            phase(0, 0, 1, with_last=False)
            with dve.Fori(1, LAST, 2) as p:
                phase(p, 1, (p + 1) // 2 + 1)
                phase(p + 1, 0, (p + 1) // 2 + 1)
            phase(LAST, LAST % 2, with_next=False)
            for c in range(NC):
                if 0 < c < len(DVE_GROUPS):
                    group_lo(LAST, DVE_GROUPS[c], LAST % 2)
                save_y(LAST, c)
            y_maximum(LAST)
            invert_y_sum(LAST)
            scale_W_hi(LAST)
            scale_W_lo(LAST)
            for pair in range(2):
                y_lo(LAST, pair)
            for k in range(4):
                residual(LAST, k)


_BN_PARAMS = ("W_b", "bn_gamma", "bn_beta", "bn_mean", "bn_var")


def kernel(**inputs):
    import numpy as _np
    import concourse.bacc as _bacc
    from concourse import mybir as _mybir
    from concourse.bass_utils import run_bass_kernel_spmd as _run

    nc = _bacc.Bacc("TRN2", target_bir_lowering=False, num_devices=1)
    arrays = {"x": _np.ascontiguousarray(inputs["x"])}
    for name in ("g_w", "theta_w", "W_w"):
        arrays[name + "T"] = _np.ascontiguousarray(_np.asarray(inputs["L0_conv_" + name]).T)
    for name in ("g_b", "theta_b"):
        arrays[name] = _np.ascontiguousarray(inputs["L0_conv_" + name])
    stacked = _np.stack([_np.asarray(inputs["L0_conv_" + name]) for name in _BN_PARAMS])
    arrays["bn_params"] = _np.ascontiguousarray(stacked.reshape(len(_BN_PARAMS), -1, P).transpose(2, 0, 1))
    aps = {n: nc.dram_tensor("in_" + n, a.shape, _mybir.dt.from_np(a.dtype), kind="ExternalInput").ap()
           for n, a in arrays.items()}
    out = nc.dram_tensor("out", arrays["x"].shape, _mybir.dt.float32, kind="ExternalOutput").ap()
    psp_nonlocal_kernel(nc, aps["x"], aps["g_wT"], aps["g_b"], aps["theta_wT"], aps["theta_b"], aps["W_wT"],
                        aps["bn_params"], out)
    r = _run(nc, [{"in_" + n: a for n, a in arrays.items()}], core_ids=[0])
    return r.results[0]["out"]
```
